# Optimizing a Trainium2 kernel written in Bass

```python
import numpy as np
import jax
import jax.numpy as jnp

def _softmax(x, axis=-1):
    return jax.nn.softmax(x, axis=axis)

def _gelu(x):
    return jax.nn.gelu(x, approximate=True)

def _silu(x):
    return jax.nn.silu(x)

def _sigmoid(x):
    return jax.nn.sigmoid(x)

def _layernorm(x, axis=-1, eps=1e-05):
    m = jnp.mean(x, axis=axis, keepdims=True)
    v = jnp.var(x, axis=axis, keepdims=True)
    return (x - m) / jnp.sqrt(v + eps)

def _scatter_add(tgt, idx, src, axis=0):
    return tgt.at[idx].add(src)

def _segment_sum(src, seg, n):
    return jax.ops.segment_sum(src, seg, n)
kernel_name = 'mk_gps_d1_gnn_r8_0d0820'

def setup_inputs(seed: int=0):
    np.random.seed(seed)
    _w = jnp.asarray

    def _rec_inputs():
        import jax
        import jax.numpy as jnp
        _gk = jax.random.key(seed)
        x = -8.776e-05 + 1 * jax.random.normal(jax.random.fold_in(_gk, 1), (1250, 512), jnp.float32)
        src = jax.random.randint(jax.random.fold_in(_gk, 2), (40000,), 0, 1250, jnp.int32)
        dst = jax.random.randint(jax.random.fold_in(_gk, 3), (40000,), 0, 1250, jnp.int32)
        _o = jnp.argsort(dst, stable=True)
        src = src[_o]
        dst = dst[_o]
        return (x, src, dst)
    x, src, dst = _rec_inputs()

    def _L0_gnn_setup():
        import jax, jax.numpy as jnp
        import numpy as np
        N_NODES = 1250
        N_EDGES = 20000
        D_IN = 512
        D_HID = 1024
        key = jax.random.key(seed)
        ks = jax.random.split(key, 8)
        feat = jax.random.normal(ks[0], (N_NODES, D_IN), dtype=jnp.float32)
        W1 = jax.random.normal(ks[1], (D_IN, D_HID), dtype=jnp.float32) * (1.0 / np.sqrt(D_IN))
        b1 = jnp.zeros((D_HID,), dtype=jnp.float32)
        W2 = jax.random.normal(ks[2], (D_HID, D_IN), dtype=jnp.float32) * (1.0 / np.sqrt(D_HID))
        b2 = jnp.zeros((D_IN,), dtype=jnp.float32)
        eps = jnp.zeros((1,), dtype=jnp.float32)
        src = jax.random.randint(ks[3], (N_EDGES,), 0, N_NODES, dtype=jnp.int32)
        dst = jax.random.randint(ks[4], (N_EDGES,), 0, N_NODES, dtype=jnp.int32)
        return {'feat': feat, 'W1': W1, 'b1': b1, 'W2': W2, 'b2': b2, 'eps': eps, 'src': src, 'dst': dst}
    _L0_gnn_all = _L0_gnn_setup()
    _L0_gnn_in = {k: v for k, v in _L0_gnn_all.items() if k in ('W1', 'b1', 'W2', 'b2', 'eps')}
    del _L0_gnn_all

    def _L0_mix_setup():
        import jax, jax.numpy as jnp
        import numpy as np
        HEADS = 8
        DIM_HEAD = 64
        SCALE = DIM_HEAD ** (-0.5)
        key = jax.random.key(seed)
        k1, k2, k3 = jax.random.split(key, 3)
        B, N, D = (2, 512, 512)
        x = jax.random.normal(k1, (B, N, D), dtype=jnp.float32)
        W_qkv = jax.random.normal(k2, (3 * HEADS * DIM_HEAD, D), dtype=jnp.float32) * D ** (-0.5)
        W_out = jax.random.normal(k3, (D, HEADS * DIM_HEAD), dtype=jnp.float32) * (HEADS * DIM_HEAD) ** (-0.5)
        b_out = jnp.zeros((D,), dtype=jnp.float32)
        return {'x': x, 'W_qkv': W_qkv, 'W_out': W_out, 'b_out': b_out}
    _L0_mix_all = _L0_mix_setup()
    _L0_mix_in = {k: v for k, v in _L0_mix_all.items() if k in ('W_qkv', 'W_out', 'b_out')}
    del _L0_mix_all

    def _L0_ffn_setup():
        import jax, jax.numpy as jnp
        import numpy as np
        from jax import lax
        N_EXPERTS = 16
        TOP_K = 2
        D_MODEL = 512
        D_FF = 256
        key = jax.random.key(seed)
        ks = jax.random.split(key, 7)
        s_in = 1.0 / np.sqrt(D_MODEL)
        s_ff = 1.0 / np.sqrt(D_FF)
        x = jax.random.normal(ks[0], (2, 256, D_MODEL), dtype=jnp.float32)
        router_w = jax.random.uniform(ks[1], (N_EXPERTS, D_MODEL), jnp.float32, -s_in, s_in)
        router_b = jax.random.uniform(ks[2], (N_EXPERTS,), jnp.float32, -s_in, s_in)
        w1 = jax.random.uniform(ks[3], (N_EXPERTS, D_FF, D_MODEL), jnp.float32, -s_in, s_in)
        b1 = jax.random.uniform(ks[4], (N_EXPERTS, D_FF), jnp.float32, -s_in, s_in)
        w2 = jax.random.uniform(ks[5], (N_EXPERTS, D_MODEL, D_FF), jnp.float32, -s_ff, s_ff)
        b2 = jax.random.uniform(ks[6], (N_EXPERTS, D_MODEL), jnp.float32, -s_ff, s_ff)
        return {'x': x, 'router_w': router_w, 'router_b': router_b, 'w1': w1, 'b1': b1, 'w2': w2, 'b2': b2}
    _L0_ffn_all = _L0_ffn_setup()
    _L0_ffn_in = {k: v for k, v in _L0_ffn_all.items() if k in ('router_w', 'router_b', 'w1', 'b1', 'w2', 'b2')}
    del _L0_ffn_all
    return {'x': x, 'src': src, 'dst': dst, 'L0_gnn_W1': _L0_gnn_in['W1'], 'L0_gnn_b1': _L0_gnn_in['b1'], 'L0_gnn_W2': _L0_gnn_in['W2'], 'L0_gnn_b2': _L0_gnn_in['b2'], 'L0_gnn_eps': _L0_gnn_in['eps'], 'L0_mix_W_qkv': _L0_mix_in['W_qkv'], 'L0_mix_W_out': _L0_mix_in['W_out'], 'L0_mix_b_out': _L0_mix_in['b_out'], 'L0_ffn_router_w': _L0_ffn_in['router_w'], 'L0_ffn_router_b': _L0_ffn_in['router_b'], 'L0_ffn_w1': _L0_ffn_in['w1'], 'L0_ffn_b1': _L0_ffn_in['b1'], 'L0_ffn_w2': _L0_ffn_in['w2'], 'L0_ffn_b2': _L0_ffn_in['b2']}

def reference(x, src, dst, L0_gnn_W1, L0_gnn_b1, L0_gnn_W2, L0_gnn_b2, L0_gnn_eps, L0_mix_W_qkv, L0_mix_W_out, L0_mix_b_out, L0_ffn_router_w, L0_ffn_router_b, L0_ffn_w1, L0_ffn_b1, L0_ffn_w2, L0_ffn_b2):
    import jax
    import jax.numpy as jnp

    def _L0_gnn_ref(feat, W1, b1, W2, b2, eps, src, dst):
        import jax, jax.numpy as jnp
        import numpy as np
        N_NODES = 1250
        N_EDGES = 20000
        D_IN = 512
        D_HID = 1024
        msgs = feat[src]
        neigh = jax.ops.segment_sum(msgs, dst, num_segments=feat.shape[0])
        rst = (1.0 + eps[0]) * feat + neigh
        h = jnp.maximum(rst @ W1 + b1, 0.0)
        h = h @ W2 + b2
        return h + feat

    def _L0_mix_ref(x, W_qkv, W_out, b_out):
        import jax, jax.numpy as jnp
        import numpy as np
        HEADS = 8
        DIM_HEAD = 64
        SCALE = DIM_HEAD ** (-0.5)
        B, N, D = x.shape
        qkv = jnp.einsum('bnd,ed->bne', x, W_qkv)
        q, k, v = jnp.split(qkv, 3, axis=-1)

        def to_heads(t):
            return t.reshape(B, N, HEADS, DIM_HEAD).transpose(0, 2, 1, 3)
        q, k, v = (to_heads(q), to_heads(k), to_heads(v))
        q = q * SCALE
        qk = jnp.einsum('bhnd,bhmd->bhnm', q, k)
        qk = jax.nn.relu(qk)
        attn = jnp.einsum('bhnm,bhmd->bhnd', qk, v)
        out = attn.transpose(0, 2, 1, 3).reshape(B, N, HEADS * DIM_HEAD)
        return jnp.einsum('bne,de->bnd', out, W_out) + b_out

    def _L0_ffn_ref(x, router_w, router_b, w1, b1, w2, b2):
        import jax, jax.numpy as jnp
        import numpy as np
        from jax import lax
        N_EXPERTS = 16
        TOP_K = 2
        D_MODEL = 512
        D_FF = 256
        B, S, D = x.shape
        xt = x.reshape(-1, D)
        logits = xt @ router_w.T + router_b
        probs = jax.nn.softmax(logits, axis=-1)
        topk_p, topk_i = lax.top_k(probs, TOP_K)
        onehot = jax.nn.one_hot(topk_i, N_EXPERTS, dtype=probs.dtype)
        gates = jnp.sum(onehot * topk_p[..., None], axis=1)

        def expert_step(acc, packed):
            w1e, b1e, w2e, b2e, ge = packed
            h = jax.nn.gelu(xt @ w1e.T + b1e, approximate=False)
            y = h @ w2e.T + b2e
            return (acc + y * ge[:, None], None)
        out, _ = lax.scan(expert_step, jnp.zeros_like(xt), (w1, b1, w2, b2, gates.T))
        return out.reshape(B, S, D)
    xn = _layernorm(x, axis=-1)
    x = x + _L0_gnn_ref(xn, L0_gnn_W1, L0_gnn_b1, L0_gnn_W2, L0_gnn_b2, L0_gnn_eps, src, dst) + _L0_mix_ref(xn[None], L0_mix_W_qkv, L0_mix_W_out, L0_mix_b_out)[0]
    x = x + _L0_ffn_ref(_layernorm(x, axis=-1)[None], L0_ffn_router_w, L0_ffn_router_b, L0_ffn_w1, L0_ffn_b1, L0_ffn_w2, L0_ffn_b2)[0]
    return x

_drawn_inputs = setup_inputs


def setup_inputs(seed=0):
    import zlib

    import numpy as np

    out = dict(_drawn_inputs(seed))
    spreads = {'L0_gnn_b1': (0.0, 2.0), 'L0_gnn_b2': (0.0, 2.0), 'L0_mix_b_out': (0.0, 2.0)}
    factors = {'L0_ffn_router_w': 8.0,
     'L0_ffn_router_b': 26.293,
     'L0_ffn_w1': 8.0,
     'L0_ffn_b1': 55.447,
     'L0_ffn_w2': 8.0,
     'L0_ffn_b2': 64.0}
    for name, (base, spread) in spreads.items():
        noise = np.random.default_rng([zlib.crc32(name.encode()), seed]).standard_normal(out[name].shape)
        drawn = base * np.exp(spread * noise) if base else spread * noise
        out[name] = jnp.asarray(drawn.astype(out[name].dtype))
    for name, factor in factors.items():
        out[name] = (out[name] * factor).astype(out[name].dtype)
    return out
```

```python
from contextlib import ExitStack

import concourse.bass as bass
from concourse import mybir

P = 128
N = 1250
D = 512
NT = 10
LAST = N - (NT - 1) * P
KD = D // P
HEADS, DH = 8, 64
PAIRS = HEADS // 2
BLOCKS = [(0, 418), (418, 416), (834, 416)]
BW = 418
HID = 1024
KH = HID // P
EDGES = 40000
CE = 125
CP = 80
CJ = 4
NC = CP * CJ
WD = 32
NW = NT * P // WD
WPG = P // WD
WCOL = NT * WD
RING = 16
SPARE = 2
OHW = P + WCOL
USUAL = [-(-EDGES * min(WD, N - w * WD) // (N * CE)) + 1 for w in range(NW)]
FIRST = [sum(USUAL[:w]) for w in range(NW + 1)]
EXP = 16
DFF = 256
KF = DFF // P
EW = KD * DFF + KF * D
MAXT = 2 * N // P + EXP + 3
EPS = 1e-5
SCALE = DH ** -0.5
FAR = 1000.0


def layer(nc, x, src, dst, wqkv, wo, bo, gw1, gb1, gw2, gb2, geps, rw, rb, ew, eb1, eb2, out):
    f32, f16, bf16, i32 = mybir.dt.float32, mybir.dt.float16, mybir.dt.bfloat16, mybir.dt.int32
    ALU = mybir.AluOpType
    ACT = mybir.ActivationFunctionType
    X = mybir.AxisListType.X

    xs = nc.dram_tensor("slots", [MAXT * P, D], f32, kind="Internal").ap()

    with ExitStack() as ctx:
        def sb(name, shape, dt=f32):
            return ctx.enter_context(nc.sbuf_tensor(name, shape, dt))

        def sem(name):
            return ctx.enter_context(nc.semaphore(name))

        ARENA = 46080
        arena = sb("arena", [P, ARENA])

        def at(a, shape, dt=None, parts=P):
            n = 1
            for s in shape:
                n *= s
            v = arena[0:parts, a:a + n]
            if len(shape) == 2:
                v = v.rearrange("p (a b) -> p a b", b=shape[1])
            if len(shape) == 3:
                v = v.rearrange("p (a b c) -> p a b c", b=shape[1], c=shape[2])
            return v

        xn = at(0, [NT, D])
        zeros = at(5120, [D])
        a_t = at(5120, [2, NT, P])
        probs = at(7680, [2, 2, BW])
        bias_b2, bias_bo = at(7680, [D]), at(7680 + D, [D])
        ring = arena[0:CE, 9352:9352 + RING * OHW // 2].bitcast(f16)
        E0 = 9352
        src_i, dst_i = (arena[0:CP, E0 + a * 500:E0 + (a + 1) * 500].bitcast(i32) for a in (0, 1))
        hi_i, lo_i, win_i, off_i = (arena[0:CP, E0 + a * 500:E0 + (a + 1) * 500].bitcast(i32)
                                    for a in (2, 3, 4, 5))
        lo_f = arena[0:CP, E0 + 3000:E0 + 3500]
        val_f = arena[0:CP, 6200:6700]
        marks = at(5700, [2, NW, CJ], parts=CP)
        marks2 = arena[0:CP, 6020:6020 + 2 * NW]
        spare = arena[0:CE, 12936:12936 + SPARE * OHW // 2].bitcast(f16)
        rst = at(13384, [D])
        NCP = NC + max(USUAL)
        val = arena[0:CE, 13896:13896 + NCP]
        low = arena[0:CE, 14226:14226 + NCP]
        xn_t = at(14848, [KD, NT * P])
        rst_t = at(14848, [KD, NT * P])
        w1 = at(19968, [KD, HID])
        q_t = at(24576, [PAIRS, N])
        k_t = at(29696, [PAIRS, NT * P])
        v = at(34816, [NT, D])
        h_t = at(29696, [KH, N])
        w_qkv = at(39936, [KD, 3 * D])
        w2 = at(39936, [KH, D])
        w_o = at(44032, [KD, D])
        E_BASE = 4096
        b1_all = arena[:, 0:EXP * DFF]
        R0 = E_BASE + 4 * EW

        def small(k, *shape):
            return at(R0 + 160 * k, list(shape))

        logits, prob, tmp, oh1, oh2, rank, gates = (small(k, NT, EXP) for k in range(7))
        total = at(R0 + 1120, [EXP])
        many = at(R0 + 1140, [EXP, NT])
        ntile = at(R0 + 1300, [EXP])
        tstart = at(R0 + 1316, [EXP])
        tend = at(R0 + 1332, [EXP])
        cum = at(R0 + 1350, [EXP, EXP])
        red = at(R0 + 1606, [NT])
        red2 = at(R0 + 1616, [NT])
        red3 = at(R0 + 1626, [NT])
        sums_red = at(R0 + 1636, [NT])
        tef = at(R0 + 1650, [MAXT])
        tcmp = at(R0 + 160 * 0, [MAXT, EXP])
        x2n = at(18432, [NT, D])
        x2n_t = at(23552, [2, KD, P])
        S = 36864
        xg = at(S, [2, D])
        xg_t = at(S + 1024, [2, KD, P])
        hb = at(S + 2048, [2, DFF])
        hg = at(S + 2560, [2, DFF])
        hg_t = at(S + 3072, [2, KF, P])
        y_sb = at(S + 3584, [2, D])
        gates_t = arena[0:EXP, S + 4608:S + 4608 + NT * P]
        yg = at(0, [2, NT, D])

        xr = sb("xr", [P, NT, D])
        ident = sb("ident", [P, P])
        iota16 = sb("iota16", [P, WCOL], f16)
        tri = sb("tri", [P, P], bf16)
        ones = sb("ones", [P, P], bf16)
        mask16 = sb("mask16", [P, NT * EXP], bf16)
        win_idx = sb("win_idx", [CP, NW])
        chunk_idx = sb("chunk_idx", [CP, CJ])
        chunk_neg = sb("chunk_neg", [CP, CJ])
        first5 = sb("first5", [CP, CJ])
        last5 = sb("last5", [CP, CJ])
        mincol = sb("mincol", [CP, 1])
        minrow = sb("minrow", [1, 2 * NW])
        bounds = sb("bounds", [1, NW, 2], i32)
        valid = sb("valid", [P, NT])
        einv = sb("einv", [P, EXP])
        thr = sb("thr", [P, NT])
        tidx = sb("tidx", [P, MAXT])
        below = sb("below", [P, EXP, EXP])
        eps_c = sb("eps_c", [P, 1])
        eps1 = sb("eps1", [P, 1])
        b1 = sb("b1", [P, KH])
        rw_sb = sb("rw_sb", [P, KD, EXP])
        rb_sb = sb("rb_sb", [P, EXP])
        b2_sb = sb("b2_sb", [EXP, D])
        stats = sb("stats", [P, NT, 6])
        mv = sb("mv", [P, NT, 2])
        std = sb("std", [P, NT])
        rstd = sb("rstd", [P, NT])
        gate = sb("gate", [P, 2, NT])
        slot = sb("slot", [P, 2, NT], i32)
        te = sb("te", [P, MAXT], i32)
        npair = sb("npair", [P, 1], i32)

        bank = [ctx.enter_context(nc.psum_tensor(f"bank{i}", [P, 512], f32)) for i in range(8)]
        AV, AW, NB, TR = 4, 5, 6, 7

        x_in = [sem(f"x_in{i}") for i in range(3)]
        edges_in, bias_in, b1_in, rw_in, rb_in, b2_in, eps_in = (
            sem(s) for s in ("edges_in", "bias_in", "b1_in", "rw_in", "rb_in", "b2_in", "eps_in"))
        wqkv_in, w1_in, w2_in, wo_in, eb1_in = (sem(s) for s in ("wqkv_in", "w1_in", "w2_in", "wo_in", "eb1_in"))
        ew_in = [sem(f"ew_in{e}") for e in range(EXP)]
        zero_filled = sem("zero_filled")
        xpad_ready, zeros_ready, pool_chain, consts_ready = (
            sem(s) for s in ("xpad_ready", "zeros_ready", "pool_chain", "consts_ready"))
        base_ready = sem("base_ready")
        dve_chain, var_ready, std_ready, xn_ready = (sem(s) for s in ("dve_chain", "var_ready", "std_ready", "xn_ready"))
        xnt_ps, xnt_saved = sem("xnt_ps"), sem("xnt_saved")
        proj_ps, proj_saved = sem("proj_ps"), sem("proj_saved")
        edge_ready, edge_ps, edge_saved, min_ps = (sem(s) for s in ("edge_ready", "edge_ps", "edge_saved", "min_ps"))
        marks_ready, mins_ps, mincol_ready, bounds_ready = (
            sem(s) for s in ("marks_ready", "mins_ps", "mincol_ready", "bounds_ready"))
        onehots_ready, onehots_used = sem("onehots_ready"), sem("onehots_used")
        spare_ready, spare_used = sem("spare_ready"), sem("spare_used")
        window_saved = sem("window_saved")
        neigh_ps, rst_ready, rstt_ps, rstt_saved = (sem(s) for s in ("neigh_ps", "rst_ready", "rstt_ps", "rstt_saved"))
        qk_ps, probs_ready, av_step, av_saved = (sem(s) for s in ("qk_ps", "probs_ready", "av_step", "av_saved"))
        hid_ps, hid_saved = sem("hid_ps"), sem("hid_saved")
        mix_ps, x2_ready = sem("mix_ps"), sem("x2_ready")
        var2_ready, std2_ready, x2n_ready, x2nt_ps, x2nt_saved, logit_ps = (
            sem(s) for s in ("var2_ready", "std2_ready", "x2n_ready", "x2nt_ps", "x2nt_saved", "logit_ps"))
        shifted_ready, exp_ready, mask_ready, rank_ps, route_ready = (
            sem(s) for s in ("shifted_ready", "exp_ready", "mask_ready", "rank_ps", "route_ready"))
        gates_ready, gt_ps, gt_saved, gb_ps, gb_added = (
            sem(s) for s in ("gates_ready", "gt_ps", "gt_saved", "gb_ps", "gb_added"))
        scattered, w_ready = sem("scattered"), sem("w_ready")
        xg_in = [sem(f"xg_in{i}") for i in range(2)]
        xgt_ps = [sem(f"xgt_ps{i}") for i in range(2)]
        xgt_saved = [sem(f"xgt_saved{i}") for i in range(2)]
        h_ps = [sem(f"h_ps{i}") for i in range(2)]
        hb_ready = [sem(f"hb_ready{i}") for i in range(2)]
        hg_ready = [sem(f"hg_ready{i}") for i in range(2)]
        hgt_ps = [sem(f"hgt_ps{i}") for i in range(2)]
        hgt_saved = [sem(f"hgt_saved{i}") for i in range(2)]
        y_ps = [sem(f"y_ps{i}") for i in range(2)]
        y_saved = [sem(f"y_saved{i}") for i in range(2)]
        y_stored = [sem(f"y_stored{i}") for i in range(2)]
        yg_in = [sem(f"yg_in{t}") for t in range(NT)]
        rows_stored, res_ready, stored = sem("rows_stored"), sem("res_ready"), sem("stored")

        def rows(t):
            return LAST if t == NT - 1 else P

        steps = [(p, b, t) for p in range(PAIRS) for b in range(len(BLOCKS)) for t in range(NT)]
        NS = len(steps)
        between = [[] for _ in range(NS)]
        for w in range(NW):
            s = 1 + (w * 11) // 4
            between[s].append(("window", w))
            if w % WPG == WPG - 1:
                g = w // WPG
                for part in range(3):
                    between[min(s + part, NS - 1)].append(("sum", g, part))
                between[min(s + 4, NS - 1)].append(("turn", g))
        PARTS = [range(0, 4), range(4, 7), range(7, 10)]

        def register_loop(eng, name, first):
            r = eng.alloc_register(name)
            eng.reg_mov(r, first)
            return r

        block = ctx.enter_context(nc.Block())

        @block.sync
        def _(sp):
            xv = x[0:(NT - 1) * P, :].rearrange("(t p) d -> p t d", p=P)
            sp.dma_start(xr[:, 0:5, :], xv[:, 0:5, :]).then_inc(x_in[0], 16)
            sp.dma_start(xr[:, 5:9, :], xv[:, 5:9, :]).then_inc(x_in[1], 16)
            sp.wait_ge(xpad_ready, 1)
            sp.dma_start(xr[0:LAST, NT - 1, :], x[(NT - 1) * P:N, :]).then_inc(x_in[2], 16)
            for k in range(KD):
                sp.dma_start(w_qkv[:, k, :], wqkv[:, k, :]).then_inc(wqkv_in, 16)
            sp.dma_start(w1[:, :, :], gw1).then_inc(w1_in, 16)
            sp.wait_ge(zeros_ready, 1)
            sp.dma_start(xs.rearrange("(t p) d -> p t d", p=P),
                         zeros.unsqueeze(1).to_broadcast([P, MAXT, D])).then_inc(zero_filled, 16)
            sp.wait_ge(proj_ps, 2 * KD * 3 + NT)
            sp.dma_start(w2[:, :, :], gw2).then_inc(w2_in, 16)
            sp.dma_start(w_o[:, :, :], wo).then_inc(wo_in, 16)

            def expert(e):
                sp.dma_start(arena[:, E_BASE + e * EW:E_BASE + (e + 1) * EW], ew[e]).then_inc(ew_in[e], 16)

            sp.wait_ge(rstt_ps, NT)
            sp.wait_ge(av_step, NS)
            sp.wait_ge(base_ready, NT)
            sp.dma_start(b1_all, eb1.partition_broadcast(P)).then_inc(eb1_in, 16)
            for e in range(4):
                expert(e)
            sp.wait_ge(hid_ps, KH * 3)
            for e in (5, 6):
                expert(e)
            sp.wait_ge(mix_ps, NT)
            for e in range(10, EXP):
                expert(e)
            sp.wait_ge(scattered, 16 * 2 * NT)
            sp.wait_ge(gt_ps, NT)
            for e in (4, 7, 8, 9):
                expert(e)
            sp.wait_ge(zero_filled, 16)
            for a in range(2):
                sp.dma_start(xg[:, a, :], xs[a * P:(a + 1) * P, :]).then_inc(xg_in[a], 16)
            n = sp.value_load(npair[0:1, 0:1], min_val=1, max_val=(MAXT - 1) // 2)
            with sp.Fori(0, n) as j:
                for a in range(2):
                    sp.wait_ge(xgt_ps[a], j + 1)
                    sp.dma_start(xg[:, a, :], xs[bass.ds((2 * j + 2 + a) * P, P), :]).then_inc(xg_in[a], 16)
                for a in range(2):
                    sp.wait_ge(y_saved[a], j + 2)
                    sp.dma_start(xs[bass.ds((2 * j + a) * P, P), :], y_sb[:, a, :]).then_inc(y_stored[a], 16)
            for a in range(2):
                sp.wait_ge(xg_in[a], 16 * (n + 1))
            for t in range(NT):
                sp.wait_ge(res_ready, t + 1)
                sp.dma_start(out[t * P:t * P + rows(t), :], xr[0:rows(t), t, :]).then_inc(stored, 16)
            sp.wait_ge(stored, 16 * NT)

        @block.gpsimd
        def _(pool):
            count = [0]

            def link(ins):
                count[0] += 1
                ins.then_inc(pool_chain, 1)
                pool.wait_ge(pool_chain, count[0])

            link(pool.memset(xr[96:P, NT - 1, :], 0.0))
            pool.sem_inc(xpad_ready, 1)
            pool.dma_start(dst_i, dst.rearrange("(p n) -> p n", p=CP)).then_inc(edges_in, 16)
            pool.dma_start(src_i, src.rearrange("(p n) -> p n", p=CP)).then_inc(edges_in, 16)
            pool.dma_start(bias_b2, gb2.partition_broadcast(P)).then_inc(bias_in, 16)
            pool.dma_start(bias_bo, bo.partition_broadcast(P)).then_inc(bias_in, 16)
            pool.dma_start(b1[:, :], gb1).then_inc(b1_in, 16)
            pool.dma_start(rw_sb[:, :, :], rw).then_inc(rw_in, 16)
            pool.dma_start(rb_sb[:, :], rb.partition_broadcast(P)).then_inc(rb_in, 16)
            pool.dma_start(eps_c[:, :], geps.partition_broadcast(P)).then_inc(eps_in, 16)
            pool.dma_start(b2_sb[:, :], eb2).then_inc(b2_in, 16)
            link(pool.memset(ident[:, :], 0.0))
            link(pool.affine_select(out=ident[:, :], in_=ident[:, :], compare_op=ALU.not_equal, fill=1.0,
                                    base=0, pattern=[[-1, P]], channel_multiplier=1))
            pool.sem_inc(consts_ready, 1)
            link(pool.memset(zeros, 0.0))
            pool.sem_inc(zeros_ready, 1)
            link(pool.memset(tri[:, :], 1.0))
            link(pool.affine_select(out=tri[:, :], in_=tri[:, :], compare_op=ALU.is_ge, fill=0.0,
                                    base=-1, pattern=[[1, P]], channel_multiplier=-1))
            link(pool.memset(valid[:, :], 1.0))
            link(pool.affine_select(out=valid[:, NT - 1:NT], in_=valid[:, NT - 1:NT], compare_op=ALU.is_ge,
                                    fill=0.0, base=LAST - 1, pattern=[[0, 1]], channel_multiplier=-1))
            link(pool.memset(below[:, :, :], 1.0))
            link(pool.affine_select(out=below[:, :, :], in_=below[:, :, :], compare_op=ALU.is_ge, fill=0.0,
                                    base=-1, pattern=[[1, EXP], [-1, EXP]], channel_multiplier=0))
            link(pool.memset(ones[:, :], 1.0))

            def ramp(t, pattern, base=0, per_partition=0):
                link(pool.iota(t, pattern=pattern, base=base, channel_multiplier=per_partition,
                               allow_small_or_imprecise_dtypes=True))

            ramp(iota16[:, :], [[1, WCOL]])
            ramp(win_idx[:, :], [[1, NW]])
            ramp(chunk_idx[:, :], [[1, CJ]], 0, CJ)
            ramp(chunk_neg[:, :], [[-1, CJ]], 0, -CJ)
            ramp(einv[:, :], [[-1, EXP]], EXP)
            ramp(thr[:, :], [[P, NT]])
            ramp(tidx[:, :], [[1, MAXT]])
            pool.sem_inc(consts_ready, 1)
            pool.wait_ge(bias_in, 32)
            link(pool.tensor_tensor(bias_b2, bias_b2, bias_bo, ALU.add))
            for t in range(NT):
                pool.wait_ge(xn_ready, t + 1)
                link(pool.tensor_tensor(xr[:, t, :], xr[:, t, :], xn[:, t, :], ALU.add))
                link(pool.tensor_tensor(xr[:, t, :], xr[:, t, :], bias_b2, ALU.add))
                pool.sem_inc(base_ready, 1)
            pool.wait_ge(route_ready, 1)
            pool.wait_ge(zero_filled, 16)
            for t in range(NT):
                for k in range(2):
                    pool.indirect_dma_start(
                        out=xs, out_offset=bass.IndirectOffsetOnAxis(ap=slot[0:rows(t), k, t:t + 1], axis=0),
                        in_=x2n[0:rows(t), t, :], in_offset=None).then_inc(scattered, 16)
            for e in range(EXP):
                pool.wait_ge(ew_in[e], 16)
                pool.sem_inc(w_ready, 1)
            n = pool.value_load(npair[0:1, 0:1], min_val=1, max_val=(MAXT - 1) // 2)
            for a in range(2):
                pool.wait_ge(y_stored[a], 16 * n + 16)
                pool.sem_inc(rows_stored, 1)
            pool.wait_ge(rows_stored, 2)
            for t in range(NT):
                for k in range(2):
                    pool.indirect_dma_start(
                        out=yg[0:rows(t), k, t, :], out_offset=None, in_=xs,
                        in_offset=bass.IndirectOffsetOnAxis(ap=slot[0:rows(t), k, t:t + 1], axis=0)
                    ).then_inc(yg_in[t], 16)

        @block.scalar
        def _(act):
            copy = ACT.Copy
            for half in range(2):
                act.wait_ge(var_ready, half + 1)
                act.activation(std[:, 5 * half:5 * half + 5], std[:, 5 * half:5 * half + 5],
                               ACT.Sqrt).then_inc(std_ready, 1)
            for t in range(NT):
                act.wait_ge(xnt_ps, t + 1)
                act.activation(xn_t[:, :, t * P:(t + 1) * P],
                               bank[6 + t % 2][:, :].rearrange("p (k n) -> p k n", k=KD),
                               copy).then_inc(xnt_saved, 1)
            g = 0
            for m in range(2 * KD):
                for o, n in BLOCKS:
                    act.wait_ge(proj_ps, g + 1)
                    dst_t = q_t if m < KD else k_t
                    act.activation(dst_t[:, m % KD, o:o + n], bank[g % 6][:, 0:n], copy).then_inc(proj_saved, 1)
                    g += 1
            for t in range(NT):
                act.wait_ge(proj_ps, g + 1)
                act.activation(v[:, t, :], bank[g % 6][:, :], copy).then_inc(proj_saved, 1)
                g += 1

            def save_attention(p, b):
                o, n = BLOCKS[b]
                act.wait_ge(av_step, NT * (p * 3 + b + 1))
                act.activation(q_t[:, p, o:o + n], bank[AV][:, 0:n], copy).then_inc(av_saved, 1)

            act.wait_ge(base_ready, NT)
            turned = 0
            for s, (p, b, t) in enumerate(steps):
                n = BLOCKS[b][1]
                kt = rows(t)
                act.wait_ge(qk_ps, s + 1)
                if s >= 2:
                    act.wait_ge(av_step, s - 1)
                for h in range(2):
                    ins = act.activation(probs[0:kt, s % 2, h, 0:n], bank[2 * (s % 2) + h][0:kt, 0:n],
                                         ACT.Relu, scale=SCALE)
                ins.then_inc(probs_ready, 1)
                if s and s % NT == 0:
                    save_attention(*steps[s - 1][0:2])
                if s:
                    for what in between[s - 1]:
                        if what[0] == "turn":
                            turned += 1
                            act.wait_ge(rstt_ps, turned)
                            act.activation(rst_t[:, :, (turned - 1) * P:turned * P],
                                           bank[TR][:, :].rearrange("p (k n) -> p k n", k=KD),
                                           copy).then_inc(rstt_saved, 1)
            save_attention(PAIRS - 1, 2)
            while turned < NT:
                turned += 1
                act.wait_ge(rstt_ps, turned)
                act.activation(rst_t[:, :, (turned - 1) * P:turned * P],
                               bank[TR][:, :].rearrange("p (k n) -> p k n", k=KD), copy).then_inc(rstt_saved, 1)
            act.wait_ge(b1_in, 16)
            g = 0
            for m in range(KH):
                for o, n in BLOCKS:
                    act.wait_ge(hid_ps, g + 1)
                    act.activation(h_t[:, m, o:o + n], bank[g % 4][:, 0:n], ACT.Relu,
                                   bias=b1[:, m:m + 1]).then_inc(hid_saved, 1)
                    g += 1
            for t in range(NT):
                act.wait_ge(var2_ready, t + 1)
                act.activation(std[:, t:t + 1], std[:, t:t + 1], ACT.Sqrt).then_inc(std2_ready, 1)
                act.wait_ge(x2nt_ps, t + 1)
                if t >= 2:
                    act.wait_ge(logit_ps, t - 1)
                act.activation(x2n_t[:, t % 2, :, :], bank[6][:, :].rearrange("p (k n) -> p k n", k=KD),
                               copy).then_inc(x2nt_saved, 1)
            act.wait_ge(shifted_ready, 1)
            act.activation(prob[:, :, :], logits[:, :, :], ACT.Exp).then_inc(exp_ready, 1)
            for t in range(NT):
                act.wait_ge(gt_ps, t + 1)
                act.activation(gates_t[:, t * P:(t + 1) * P], bank[t % 2][0:EXP, 0:P], copy).then_inc(gt_saved, 1)
            for a in range(2):
                act.wait_ge(xgt_ps[a], 1)
                act.activation(xg_t[:, a, :, :], bank[4 + a][:, :].rearrange("p (k n) -> p k n", k=KD),
                               copy).then_inc(xgt_saved[a], 1)
            n = act.value_load(npair[0:1, 0:1], min_val=1, max_val=(MAXT - 1) // 2)
            with act.Fori(0, n) as j:
                for a in range(2):
                    act.wait_ge(hb_ready[a], j + 2)
                    act.activation(hg[:, a, :], hb[:, a, :], ACT.Gelu).then_inc(hg_ready[a], 1)
                for a in range(2):
                    act.wait_ge(xgt_ps[a], j + 2)
                    act.activation(xg_t[:, a, :, :], bank[4 + a][:, :].rearrange("p (k n) -> p k n", k=KD),
                                   copy).then_inc(xgt_saved[a], 1)

        @block.vector
        def _(dve):
            count = [0]

            def link(ins):
                count[0] += 1
                ins.then_inc(dve_chain, 1)
                dve.wait_ge(dve_chain, count[0])

            for half in range(2):
                for t in range(5 * half, 5 * half + 5):
                    if t == 0:
                        dve.wait_ge(x_in[0], 16)
                    if t == 5:
                        dve.wait_ge(x_in[1], 16)
                    if t == NT - 1:
                        dve.wait_ge(x_in[2], 16)
                        dve.wait_ge(xpad_ready, 1)
                    ins = dve.bn_stats(stats[:, t, :], xr[:, t, :])
                link(ins)
                for t in range(5 * half, 5 * half + 5):
                    ins = dve.bn_aggr(mv[:, t, :], stats[:, t, :])
                link(ins)
                dve.tensor_scalar_add(std[:, 5 * half:5 * half + 5], mv[:, 5 * half:5 * half + 5, 1],
                                      EPS).then_inc(var_ready, 1)
                dve.wait_ge(std_ready, half + 1)
                link(dve.reciprocal(rstd[:, 5 * half:5 * half + 5], std[:, 5 * half:5 * half + 5]))
                for t in range(5 * half, 5 * half + 5):
                    dve.tensor_scalar(xn[:, t, :], xr[:, t, :], mv[:, t, 0:1], rstd[:, t:t + 1],
                                      ALU.subtract, ALU.mult).then_inc(xn_ready, 1)
            dve.wait_ge(edges_in, 32)
            dve.wait_ge(consts_ready, 2)
            dve.tensor_single_scalar(win_i, dst_i, 5, op=ALU.arith_shift_right)
            dve.tensor_single_scalar(off_i, dst_i, WD - 1, op=ALU.bitwise_and)
            dve.tensor_single_scalar(hi_i, src_i, 7, op=ALU.arith_shift_right)
            link(dve.tensor_single_scalar(lo_i, src_i, P - 1, op=ALU.bitwise_and))
            dve.tensor_copy(lo_f, lo_i).then_inc(edge_ready, 1)
            win_v = win_i.rearrange("p (j n) -> p j n", j=CJ)
            dve.tensor_reduce(first5[:, :], win_v, X, ALU.min)
            dve.tensor_reduce(last5[:, :], win_v, X, ALU.max)
            link(dve.scalar_tensor_tensor(out=val_f, in0=win_i, scalar=float(NT), in1=hi_i,
                                          op0=ALU.mult, op1=ALU.add))
            dve.scalar_tensor_tensor(out=val_f, in0=val_f, scalar=float(WD), in1=off_i,
                                     op0=ALU.mult, op1=ALU.add).then_inc(edge_ready, 1)
            for jj in range(CJ):
                dve.tensor_scalar(marks[:, 0, :, jj], win_idx[:, :], last5[:, jj:jj + 1], FAR, ALU.is_gt, ALU.mult)
                last = dve.tensor_scalar(marks[:, 1, :, jj], win_idx[:, :], first5[:, jj:jj + 1], FAR,
                                         ALU.is_lt, ALU.mult)
            link(last)
            for jj in range(CJ):
                dve.tensor_scalar(marks[:, 0, :, jj], marks[:, 0, :, jj], chunk_idx[:, jj:jj + 1], None, ALU.add)
                last = dve.tensor_scalar(marks[:, 1, :, jj], marks[:, 1, :, jj], chunk_neg[:, jj:jj + 1], None,
                                         ALU.add)
            link(last)
            dve.tensor_reduce(marks2, marks.rearrange("p a w j -> p (a w) j"), X, ALU.min).then_inc(marks_ready, 1)
            dve.wait_ge(mins_ps, 1)
            dve.tensor_reduce(mincol[:, :], bank[AW][0:2 * NW, 0:CP], X, ALU.min).then_inc(mincol_ready, 1)
            dve.wait_ge(min_ps, 1)
            link(dve.tensor_copy(minrow[:, :], bank[NB][0:1, 0:2 * NW]))
            link(dve.tensor_scalar(minrow[:, 0:NW], minrow[:, 0:NW], float(NC - 1), None, ALU.min))
            link(dve.tensor_scalar(minrow[:, NW:2 * NW], minrow[:, NW:2 * NW], -1.0, None, ALU.mult))
            link(dve.tensor_tensor(minrow[:, NW:2 * NW], minrow[:, NW:2 * NW], minrow[:, 0:NW], ALU.max))
            dve.tensor_copy(bounds[:, :, 0], minrow[:, 0:NW])
            dve.tensor_scalar(bounds[:, :, 1], minrow[:, NW:2 * NW], 1.0, None, ALU.add).then_inc(bounds_ready, 1)
            dve.wait_ge(edge_ps, 1)
            dve.tensor_copy(low[:, 0:NC].rearrange("p (c j) -> p j c", j=CJ),
                            bank[AW][0:CE, 0:NC].rearrange("p (j c) -> p j c", j=CJ)).then_inc(edge_saved, 1)
            dve.wait_ge(edge_ps, 2)
            link(dve.tensor_copy(val[:, 0:NC].rearrange("p (c j) -> p j c", j=CJ),
                                 bank[NB][0:CE, 0:NC].rearrange("p (j c) -> p j c", j=CJ)))
            dve.sem_inc(edge_saved, 1)

            dve.wait_ge(eps_in, 16)
            link(dve.tensor_scalar_add(eps1[:, :], eps_c[:, :], 1.0))
            dve.wait_ge(bounds_ready, 1)
            dve.wait_ge(zero_filled, 16)
            dve.memset(val[:, NC:NCP], -1e6)
            link(dve.memset(low[:, NC:NCP], 0.0))
            pairs = register_loop(dve, "dve_pairs", 0)

            def onehots(to, at_slot, c, ready):
                dve.tensor_scalar(to[:, bass.ds(at_slot, P)], iota16[0:CE, 0:P],
                                  low[:, bass.ds(c, 1)], None, ALU.is_equal)
                dve.tensor_scalar(to[:, bass.ds(at_slot + P, WCOL)], iota16[0:CE, :],
                                  val[:, bass.ds(c, 1)], None, ALU.is_equal).then_inc(ready, 1)

            def sums(g):
                dve.wait_ge(neigh_ps, g + 1)
                if g >= 1:
                    dve.wait_ge(rstt_ps, g)
                dve.scalar_tensor_tensor(out=rst, in0=xn[:, g, :], scalar=eps1[:, 0:1], in1=bank[NB][:, :],
                                         op0=ALU.mult, op1=ALU.add).then_inc(rst_ready, 1)

            for w in range(NW):
                if w:
                    link(dve.tensor_scalar(val, val, float(-WCOL), None, ALU.add))
                lo = dve.value_load(bounds[0:1, w, 0:1], min_val=0, max_val=NC - 1)
                hi = dve.value_load(bounds[0:1, w, 1:2], min_val=1, max_val=NC)
                for k in range(USUAL[w]):
                    i = FIRST[w] + k
                    if i >= RING:
                        dve.wait_ge(onehots_used, i - RING + 1)
                    onehots(ring, (i % RING) * OHW, lo + k, onehots_ready)
                with dve.If(lo + USUAL[w] < hi):
                    with dve.Fori(lo + USUAL[w], hi) as c:
                        i = dve.snap(pairs, min_val=0, max_val=NW * NC)
                        dve.wait_ge(spare_used, i + 1)
                        onehots(spare, (i & (SPARE - 1)) * OHW, c, spare_ready)
                        dve.reg_add(pairs, pairs, 1)
                g = w // WPG
                dve.wait_ge(onehots_used, FIRST[w + 1])
                if w % WPG == 0 and g >= 2:
                    dve.wait_ge(neigh_ps, g - 1)
                o = (w % WPG) * WD
                dve.tensor_copy(a_t[:, g % 2, :, o:o + WD],
                                bank[AW][:, 0:WCOL].rearrange("p (b d) -> p b d", b=NT)).then_inc(window_saved, 1)
                if w % WPG == 0 and g >= 1:
                    sums(g - 1)
            sums(NT - 1)

            for t in range(NT):
                r = rows(t)
                if t == 0:
                    dve.wait_ge(base_ready, NT)
                dve.wait_ge(mix_ps, t + 1)
                link(dve.tensor_tensor(xr[0:r, t, :], xr[0:r, t, :], bank[4 + t % 2][0:r, :], ALU.add))
                dve.sem_inc(x2_ready, 1)
                link(dve.bn_stats(stats[:, t, :], xr[:, t, :]))
                link(dve.bn_aggr(mv[:, t, :], stats[:, t, :]))
                dve.tensor_scalar_add(std[:, t:t + 1], mv[:, t, 1:2], EPS).then_inc(var2_ready, 1)
                dve.wait_ge(std2_ready, t + 1)
                link(dve.reciprocal(rstd[:, t:t + 1], std[:, t:t + 1]))
                if t == 0:
                    dve.wait_ge(hid_ps, KH * 3)
                dve.tensor_scalar(x2n[:, t, :], xr[:, t, :], mv[:, t, 0:1], rstd[:, t:t + 1],
                                  ALU.subtract, ALU.mult).then_inc(x2n_ready, 1)

            def over_e(a):
                return a.unsqueeze(2).to_broadcast([P, NT, EXP])

            def over_t(a):
                return a.unsqueeze(1).to_broadcast([P, NT, EXP])

            dve.wait_ge(logit_ps, NT)
            dve.wait_ge(rb_in, 16)
            lg_ps = bank[7][:, 0:NT * EXP].rearrange("p (t e) -> p t e", e=EXP)
            link(dve.tensor_tensor(logits, lg_ps, over_t(rb_sb[:, :]), ALU.add))
            link(dve.tensor_reduce(red, logits, X, ALU.max))
            dve.tensor_tensor(logits, logits, over_e(red), ALU.subtract).then_inc(shifted_ready, 1)
            dve.wait_ge(exp_ready, 1)
            link(dve.tensor_reduce(red2, prob, X, ALU.add))
            link(dve.reciprocal(red3, red2))
            link(dve.tensor_tensor(prob, prob, over_e(red3), ALU.mult))
            for k, oh in ((0, oh1), (1, oh2)):
                link(dve.tensor_reduce(gate[:, k, :], prob, X, ALU.max))
                link(dve.tensor_tensor(tmp, prob, over_e(gate[:, k, :]), ALU.is_equal))
                link(dve.tensor_tensor(tmp, tmp, over_t(einv[:, :]), ALU.mult))
                link(dve.tensor_reduce(red, tmp, X, ALU.max))
                link(dve.tensor_tensor(oh, over_t(einv[:, :]), over_e(red), ALU.is_equal))
                if k == 0:
                    link(dve.scalar_tensor_tensor(out=prob, in0=oh1, scalar=-2.0, in1=prob,
                                                  op0=ALU.mult, op1=ALU.add))
            link(dve.tensor_tensor(tmp, oh1, oh2, ALU.add))
            mask_v = mask16[:, :].rearrange("p (t e) -> p t e", e=EXP)
            link(dve.tensor_tensor(mask_v, tmp, over_e(valid[:, :]), ALU.mult))
            dve.sem_inc(mask_ready, 1)
            dve.tensor_tensor(tmp, oh1, over_e(gate[:, 0, :]), ALU.mult)
            link(dve.tensor_tensor(gates, oh2, over_e(gate[:, 1, :]), ALU.mult))
            link(dve.tensor_tensor(gates, gates, tmp, ALU.add))
            dve.sem_inc(gates_ready, 1)
            dve.wait_ge(rank_ps, 1)
            link(dve.tensor_copy(total, bank[3][:, 0:EXP]))
            link(dve.tensor_tensor(many, total.unsqueeze(2).to_broadcast([P, EXP, NT]),
                                   thr[:, :].unsqueeze(1).to_broadcast([P, EXP, NT]), ALU.is_gt))
            link(dve.tensor_reduce(ntile, many, X, ALU.add))
            link(dve.tensor_tensor(cum, ntile.unsqueeze(1).to_broadcast([P, EXP, EXP]), below[:, :, :], ALU.mult))
            link(dve.tensor_reduce(tstart, cum, X, ALU.add))
            dve.tensor_tensor(tend, tstart, ntile, ALU.add)
            link(dve.tensor_scalar(total, tstart, float(P), None, ALU.mult))
            link(dve.tensor_tensor(rank, bank[2][:, 0:NT * EXP].rearrange("p (t e) -> p t e", e=EXP),
                                   over_t(total), ALU.add))
            for k, oh in ((0, oh1), (1, oh2)):
                link(dve.tensor_tensor(tmp, oh, rank, ALU.mult))
                s_k = (sums_red, red3)[k]
                link(dve.tensor_reduce(s_k, tmp, X, ALU.add))
                last = dve.tensor_copy(slot[:, k, :], s_k)
            link(last)
            link(dve.tensor_scalar(red2[:, 0:1], tend[:, EXP - 1:EXP], 1.0, None, ALU.add))
            link(dve.tensor_copy(npair[:, :], red2[:, 0:1]))
            link(dve.tensor_single_scalar(npair[:, :], npair[:, :], 1, op=ALU.arith_shift_right))
            link(dve.tensor_tensor(tcmp, tidx[:, :].unsqueeze(2).to_broadcast([P, MAXT, EXP]),
                                   tend.unsqueeze(1).to_broadcast([P, MAXT, EXP]), ALU.is_ge))
            link(dve.tensor_reduce(tef, tcmp, X, ALU.add))
            link(dve.tensor_scalar(te[:, :], tef, float(EXP - 1), None, ALU.min))
            dve.sem_inc(route_ready, 1)
            for t in range(NT):
                r = rows(t)
                dve.wait_ge(gb_ps, t + 1)
                dve.tensor_tensor(xr[0:r, t, :], xr[0:r, t, :], bank[2 + t % 2][0:r, :], ALU.add).then_inc(gb_added, 1)
            dve.wait_ge(eb1_in, 16)
            for a in range(2):
                dve.sem_inc(hb_ready[a], 1)
                dve.sem_inc(hgt_saved[a], 1)
                dve.sem_inc(y_saved[a], 1)
                dve.sem_inc(y_stored[a], 16)
            n = dve.value_load(npair[0:1, 0:1], min_val=1, max_val=(MAXT - 1) // 2)
            with dve.Fori(0, n) as j:
                for a in range(2):
                    e = dve.value_load(te[0:1, bass.ds(2 * j + a, 1)], min_val=0, max_val=EXP - 1)
                    dve.wait_ge(h_ps[a], j + 1)
                    dve.tensor_tensor(hb[:, a, :], bank[a][:, 0:DFF], b1_all[:, bass.ds(e * DFF, DFF)],
                                      ALU.add).then_inc(hb_ready[a], 1)
                for a in range(2):
                    dve.wait_ge(hgt_ps[a], j + 1)
                    dve.tensor_copy(hg_t[:, a, :, :],
                                    bank[2 + a][:, 0:KF * P].rearrange("p (k n) -> p k n", k=KF)
                                    ).then_inc(hgt_saved[a], 1)
                for a in range(2):
                    dve.wait_ge(y_ps[a], j + 1)
                    dve.wait_ge(y_stored[a], 16 * j + 16)
                    dve.tensor_copy(y_sb[:, a, :], bank[6 + a][:, :]).then_inc(y_saved[a], 1)
            for t in range(NT):
                r = rows(t)
                dve.wait_ge(yg_in[t], 32)
                link(dve.scalar_tensor_tensor(out=xr[0:r, t, :], in0=yg[0:r, 0, t, :], scalar=gate[0:r, 0, t:t + 1],
                                              in1=xr[0:r, t, :], op0=ALU.mult, op1=ALU.add))
                dve.scalar_tensor_tensor(out=xr[0:r, t, :], in0=yg[0:r, 1, t, :], scalar=gate[0:r, 1, t:t + 1],
                                         in1=xr[0:r, t, :], op0=ALU.mult, op1=ALU.add).then_inc(res_ready, 1)

        @block.tensor
        def _(pe):
            pe.sem_inc(spare_used, SPARE)
            pe.wait_ge(consts_ready, 2)
            for t in range(NT):
                pe.wait_ge(xn_ready, t + 1)
                if t >= 2:
                    pe.wait_ge(xnt_saved, t - 1)
                for k in range(KD):
                    ins = pe.transpose(bank[6 + t % 2][:, k * P:(k + 1) * P], xn[:, t, k * P:(k + 1) * P], ident[:, :])
                ins.then_inc(xnt_ps, 1)
            pe.wait_ge(xnt_saved, NT)
            pe.wait_ge(wqkv_in, 16 * KD)
            g = 0
            for m in range(2 * KD):
                for o, n in BLOCKS:
                    if g >= 6:
                        pe.wait_ge(proj_saved, g - 5)
                    for k in range(KD):
                        ins = pe.matmul(bank[g % 6][:, 0:n], w_qkv[:, k, m * P:(m + 1) * P], xn_t[:, k, o:o + n],
                                        start=(k == 0), stop=(k == KD - 1))
                    ins.then_inc(proj_ps, 1)
                    g += 1
            for t in range(NT):
                pe.wait_ge(proj_saved, g - 5)
                for k in range(KD):
                    ins = pe.matmul(bank[g % 6][:, :], xn_t[:, k, t * P:(t + 1) * P], w_qkv[:, k, 2 * D:3 * D],
                                    start=(k == 0), stop=(k == KD - 1))
                ins.then_inc(proj_ps, 1)
                g += 1
            pe.wait_ge(proj_saved, g)
            pe.wait_ge(marks_ready, 1)
            pe.transpose(bank[AW][0:2 * NW, 0:CP], marks2, ident[0:CP, 0:CP]).then_inc(mins_ps, 1)
            pe.wait_ge(mincol_ready, 1)
            pe.transpose(bank[NB][0:1, 0:CP], mincol[:, :], ident[0:CP, 0:CP]).then_inc(min_ps, 1)
            pe.wait_ge(bounds_ready, 1)
            pe.wait_ge(edge_ready, 2)
            for a, (bk, t) in enumerate(((AW, lo_f), (NB, val_f))):
                for jj in range(CJ):
                    ins = pe.transpose(bank[bk][0:CE, jj * CP:(jj + 1) * CP], t[:, jj * CE:(jj + 1) * CE],
                                       ident[0:CP, 0:CP])
                ins.then_inc(edge_ps, 1)
            pe.wait_ge(edge_saved, 2)
            pairs = register_loop(pe, "pe_pairs", 0)

            def window(w):
                lo = pe.value_load(bounds[0:1, w, 0:1], min_val=0, max_val=NC - 1)
                hi = pe.value_load(bounds[0:1, w, 1:2], min_val=1, max_val=NC)
                if w:
                    pe.wait_ge(window_saved, w)

                def count_pair(of, at_slot, start, stop):
                    return pe.matmul(bank[AW][:, 0:WCOL], of[:, bass.ds(at_slot, P)], of[:, bass.ds(at_slot + P, WCOL)],
                                     start=start, stop=stop, skip_group_check=True)

                for k in range(USUAL[w]):
                    i = FIRST[w] + k
                    if k == USUAL[w] - 1:
                        with pe.If(lo + USUAL[w] < hi):
                            with pe.Fori(lo + USUAL[w], hi):
                                j = pe.snap(pairs, min_val=0, max_val=NW * NC)
                                pe.wait_ge(spare_ready, j + 1)
                                count_pair(spare, (j & (SPARE - 1)) * OHW, False, False).then_inc(spare_used, 1)
                                pe.reg_add(pairs, pairs, 1)
                    pe.wait_ge(onehots_ready, i + 1)
                    last = count_pair(ring, (i % RING) * OHW, k == 0, k == USUAL[w] - 1)
                    last.then_inc(onehots_used, 1)

            def neighbours(g, part):
                if part == 0:
                    pe.wait_ge(window_saved, WPG * (g + 1))
                    if g:
                        pe.wait_ge(rst_ready, g)
                for t in PARTS[part]:
                    ins = pe.matmul(bank[NB][:, :], a_t[:, g % 2, t, :], xn[:, t, :], start=(t == 0), stop=(t == NT - 1))
                if part == 2:
                    ins.then_inc(neigh_ps, 1)

            def turn(g):
                pe.wait_ge(rst_ready, g + 1)
                if g:
                    pe.wait_ge(rstt_saved, g)
                for k in range(KD):
                    ins = pe.transpose(bank[TR][:, k * P:(k + 1) * P], rst[:, k * P:(k + 1) * P], ident[:, :])
                ins.then_inc(rstt_ps, 1)

            def scores(s):
                p, b, t = steps[s]
                o, n = BLOCKS[b]
                kt = rows(t)
                if s >= 2:
                    pe.wait_ge(probs_ready, s - 1)
                for h in range(2):
                    ins = pe.matmul(bank[2 * (s % 2) + h][0:kt, 0:n], k_t[DH * h:DH * h + DH, p, t * P:t * P + kt],
                                    q_t[DH * h:DH * h + DH, p, o:o + n], start=True, stop=True)
                ins.then_inc(qk_ps, 1)

            scores(0)
            for s, (p, b, t) in enumerate(steps):
                if s + 1 < NS:
                    scores(s + 1)
                n = BLOCKS[b][1]
                kt = rows(t)
                pe.wait_ge(probs_ready, s + 1)
                if t == 0 and s:
                    pe.wait_ge(av_saved, s // NT)
                for h in range(2):
                    c = (2 * p + h) * DH
                    ins = pe.matmul(bank[AV][DH * h:DH * h + DH, 0:n], v[0:kt, t, c:c + DH], probs[0:kt, s % 2, h, 0:n],
                                    start=(t == 0), stop=(t == NT - 1))
                ins.then_inc(av_step, 1)
                for what in between[s]:
                    {"window": window, "sum": neighbours, "turn": turn}[what[0]](*what[1:])

            pe.wait_ge(rstt_saved, NT)
            pe.wait_ge(w1_in, 16)
            g = 0
            for m in range(KH):
                for o, n in BLOCKS:
                    if g >= 4:
                        pe.wait_ge(hid_saved, g - 3)
                    for k in range(KD):
                        ins = pe.matmul(bank[g % 4][:, 0:n], w1[:, k, m * P:(m + 1) * P], rst_t[:, k, o:o + n],
                                        start=(k == 0), stop=(k == KD - 1))
                    ins.then_inc(hid_ps, 1)
                    g += 1

            def mix(t):
                r = rows(t)
                if t >= 2:
                    pe.wait_ge(x2_ready, t - 1)
                for m in range(KH):
                    pe.matmul(bank[4 + t % 2][0:r, :], h_t[:, m, t * P:t * P + r], w2[:, m, :], start=(m == 0), stop=False)
                for p in range(PAIRS):
                    ins = pe.matmul(bank[4 + t % 2][0:r, :], q_t[:, p, t * P:t * P + r], w_o[:, p, :],
                                    start=False, stop=(p == PAIRS - 1))
                ins.then_inc(mix_ps, 1)

            def turn_x2n(t):
                pe.wait_ge(x2n_ready, t + 1)
                if t:
                    pe.wait_ge(x2nt_saved, t)
                for k in range(KD):
                    ins = pe.transpose(bank[6][:, k * P:(k + 1) * P], x2n[:, t, k * P:(k + 1) * P], ident[:, :])
                ins.then_inc(x2nt_ps, 1)

            def route(t):
                pe.wait_ge(x2nt_saved, t + 1)
                for k in range(KD):
                    ins = pe.matmul(bank[7][:, t * EXP:(t + 1) * EXP], x2n_t[:, t % 2, k, :], rw_sb[:, k, :],
                                    start=(k == 0), stop=(k == KD - 1))
                ins.then_inc(logit_ps, 1)

            pe.wait_ge(hid_saved, g)
            pe.wait_ge(av_saved, PAIRS * 3)
            pe.wait_ge(w2_in, 16)
            pe.wait_ge(wo_in, 16)
            pe.wait_ge(rw_in, 16)
            for t in range(NT + 2):
                if t < NT:
                    mix(t)
                if 0 <= t - 1 < NT:
                    turn_x2n(t - 1)
                if t >= 2:
                    route(t - 2)
            pe.wait_ge(mask_ready, 1)
            pe.matmul(bank[2][:, 0:NT * EXP], tri[:, :], mask16[:, :], start=True, stop=False, skip_group_check=True)
            for d in range(1, NT):
                pe.matmul(bank[2][:, d * EXP:NT * EXP], ones[:, :], mask16[:, 0:(NT - d) * EXP],
                          start=False, stop=(d == NT - 1), skip_group_check=True)
            for t in range(NT):
                ins = pe.matmul(bank[3][:, 0:EXP], ones[:, :], mask16[:, t * EXP:(t + 1) * EXP],
                                start=(t == 0), stop=(t == NT - 1))
            ins.then_inc(rank_ps, 1)
            pe.wait_ge(gates_ready, 1)
            for t in range(NT):
                if t >= 2:
                    pe.wait_ge(gt_saved, t - 1)
                pe.transpose(bank[t % 2][0:EXP, 0:P], gates[:, t, :], ident[:, :]).then_inc(gt_ps, 1)
            pe.wait_ge(route_ready, 1)
            pe.wait_ge(b2_in, 16)
            for t in range(NT):
                r = rows(t)
                pe.wait_ge(gt_saved, t + 1)
                if t >= 2:
                    pe.wait_ge(gb_added, t - 1)
                pe.matmul(bank[2 + t % 2][0:r, :], gates_t[:, t * P:t * P + r], b2_sb[:, :],
                          start=True, stop=True).then_inc(gb_ps, 1)
            pe.wait_ge(gb_added, NT)

            def turn_rows(a):
                for k in range(KD):
                    ins = pe.transpose(bank[4 + a][:, k * P:(k + 1) * P], xg[:, a, k * P:(k + 1) * P], ident[:, :])
                ins.then_inc(xgt_ps[a], 1)

            for a in range(2):
                pe.wait_ge(xg_in[a], 16)
                turn_rows(a)
            n = pe.value_load(npair[0:1, 0:1], min_val=1, max_val=(MAXT - 1) // 2)
            with pe.Fori(0, n) as j:
                e = [pe.value_load(te[0:1, bass.ds(2 * j + a, 1)], min_val=0, max_val=EXP - 1) for a in range(2)]
                for a in range(2):
                    pe.wait_ge(w_ready, e[a] + 1)
                    pe.wait_ge(xgt_saved[a], j + 1)
                    pe.wait_ge(hb_ready[a], j + 1)
                    for k in range(KD):
                        ins = pe.matmul(bank[a][:, 0:DFF], xg_t[:, a, k, :],
                                        arena[:, bass.ds(e[a] * EW + E_BASE + k * DFF, DFF)],
                                        start=(k == 0), stop=(k == KD - 1))
                    ins.then_inc(h_ps[a], 1)
                for a in range(2):
                    pe.wait_ge(hg_ready[a], j + 1)
                    pe.wait_ge(hgt_saved[a], j + 1)
                    for k in range(KF):
                        ins = pe.transpose(bank[2 + a][:, k * P:(k + 1) * P], hg[:, a, k * P:(k + 1) * P], ident[:, :])
                    ins.then_inc(hgt_ps[a], 1)
                    pe.wait_ge(xg_in[a], 16 * (j + 2))
                    pe.wait_ge(xgt_saved[a], j + 1)
                    turn_rows(a)
                for a in range(2):
                    pe.wait_ge(hgt_saved[a], j + 2)
                    pe.wait_ge(y_saved[a], j + 1)
                    for k in range(KF):
                        ins = pe.matmul(bank[6 + a][:, :], hg_t[:, a, k, :],
                                        arena[:, bass.ds(e[a] * EW + E_BASE + KD * DFF + k * D, D)],
                                        start=(k == 0), stop=(k == KF - 1))
                    ins.then_inc(y_ps[a], 1)


def kernel(x, src, dst, L0_gnn_W1, L0_gnn_b1, L0_gnn_W2, L0_gnn_b2, L0_gnn_eps, L0_mix_W_qkv, L0_mix_W_out,
           L0_mix_b_out, L0_ffn_router_w, L0_ffn_router_b, L0_ffn_w1, L0_ffn_b1, L0_ffn_w2, L0_ffn_b2):
    import numpy as np
    import concourse.bacc as bacc
    from concourse.bass_utils import run_bass_kernel_spmd

    def by_partition(w):
        w = np.asarray(w)
        return np.ascontiguousarray(w.reshape(-1, P, w.shape[1]).transpose(1, 0, 2))

    w1t = np.asarray(L0_ffn_w1).transpose(0, 2, 1).reshape(EXP, KD, P, DFF).transpose(0, 2, 1, 3).reshape(EXP, P, -1)
    w2t = np.asarray(L0_ffn_w2).transpose(0, 2, 1).reshape(EXP, KF, P, D).transpose(0, 2, 1, 3).reshape(EXP, P, -1)
    arrays = {
        "x": x, "src": src, "dst": dst,
        "wqkv": by_partition(np.asarray(L0_mix_W_qkv).T), "wo": by_partition(np.asarray(L0_mix_W_out).T),
        "bo": L0_mix_b_out, "gw1": by_partition(L0_gnn_W1), "gb1": np.asarray(L0_gnn_b1).reshape(KH, P).T,
        "gw2": by_partition(L0_gnn_W2), "gb2": L0_gnn_b2, "geps": L0_gnn_eps,
        "rw": by_partition(np.asarray(L0_ffn_router_w).T), "rb": L0_ffn_router_b,
        "ew": np.concatenate([w1t, w2t], axis=2), "eb1": np.asarray(L0_ffn_b1).reshape(-1), "eb2": L0_ffn_b2,
    }
    arrays = {f"in_{k}": np.ascontiguousarray(a) for k, a in arrays.items()}
    nc = bacc.Bacc("TRN2", target_bir_lowering=False, num_devices=1)
    args = [nc.dram_tensor(k, a.shape, mybir.dt.from_np(a.dtype), kind="ExternalInput").ap() for k, a in arrays.items()]
    out = nc.dram_tensor("out", (N, D), mybir.dt.float32, kind="ExternalOutput").ap()
    layer(nc, *args, out)
    r = run_bass_kernel_spmd(nc, [arrays], core_ids=[0])
    return r.results[0]["out"]
```

```python
from contextlib import ExitStack

import concourse.bass as bass
from concourse import mybir

P = 128
N = 1250
D = 512
NT = 10
LAST = N - (NT - 1) * P
KD = D // P
HEADS, DH = 8, 64
PAIRS = HEADS // 2
BLOCKS = [(0, 418), (418, 416), (834, 416)]
BW = 418
HID = 1024
KH = HID // P
EDGES = 40000
CE = 125
CP = 80
CJ = 4
NC = CP * CJ
WD = 32
NW = NT * P // WD
WPG = P // WD
WCOL = NT * WD
RING = 15
WBUF = 4
OHW = P + WCOL
USUAL = [-(-EDGES * min(WD, N - w * WD) // (N * CE)) + 1 for w in range(NW)]
FIRST = [sum(USUAL[:w]) for w in range(NW + 1)]
EXP = 16
DFF = 256
KF = DFF // P
EW = KD * DFF + KF * D
MAXT = 2 * N // P + EXP + 3
EPS = 1e-5
SCALE = DH ** -0.5
FAR = 1000.0


def layer(nc, x, src, dst, wqkv, wo, bo, gw1, gb1, gw2, gb2, geps, rw, rb, ew, eb1, eb2, out):
    f32r = mybir.dt.float32r
    f32, f16, bf16, i32 = mybir.dt.float32, mybir.dt.float16, mybir.dt.bfloat16, mybir.dt.int32
    ALU = mybir.AluOpType
    ACT = mybir.ActivationFunctionType
    X = mybir.AxisListType.X

    xs = nc.dram_tensor("slots", [MAXT * P, D], f32, kind="Internal").ap()

    with ExitStack() as ctx:
        def sb(name, shape, dt=f32):
            return ctx.enter_context(nc.sbuf_tensor(name, shape, dt))

        def sem(name):
            return ctx.enter_context(nc.semaphore(name))

        SLAB = 198848
        SLAB_AT = -(-nc.sbuf_base // 32) * 32
        arena = sb("arena", [P, SLAB // 4])

        def at(a, shape, parts=P):
            n = 1
            for s in shape:
                n *= s
            v = arena[0:parts, a // 4:a // 4 + n]
            if len(shape) == 2:
                v = v.rearrange("p (a b) -> p a b", b=shape[1])
            if len(shape) == 3:
                v = v.rearrange("p (a b c) -> p a b c", b=shape[1], c=shape[2])
            return v

        def split_tensor(name, a, shape):
            return nc.alloc_sbuf_tensor_at(name, [P] + shape, f32r, offset=SLAB_AT + a, align_bytes=8)

        A_T, RINGB, VALB = 0, 10240, 24576
        XN, RSTT, SET0 = 27216, 47696, 68176
        SETB = 3 * 4 * N + 120
        TMPK = SET0 + SETB
        SET1 = 88416
        PROBS = SET1 + SETB
        NPB = 3
        RSTB = PROBS + NPB * 2 * 4 * BW
        SPAREB = RSTB + 4 * D
        QT, KT, VT = 117408, 137408, 157888
        xn = at(XN, [NT, D])
        zeros = at(A_T, [D])
        a_t = at(A_T, [2, NT, P])
        marks = at(A_T + 2400, [2, NW, CJ], parts=CP)
        marks2 = at(A_T + 3700, [2 * NW], parts=CP)
        val_f = at(A_T + 4400, [500], parts=CP)
        ring = at(RINGB, [RING * OHW // 2], parts=CE).bitcast(f16)
        src_i, dst_i, hi_i, lo_i, win_i, off_i = (
            at(RINGB + 2000 * a, [500], parts=CP).bitcast(i32) for a in range(6))
        lo_f = at(RINGB + 12000, [500], parts=CP)
        NCP = NC + max(USUAL)
        window_cols = at(RINGB + RING * OHW * 2, [WBUF, 2, max(USUAL)], parts=CE)
        val = at(VALB, [NCP], parts=CE)
        low = at(VALB + 4 * NCP, [NCP], parts=CE)
        edge_cols = at(VALB, [2, NCP], parts=CE)
        xn_t = at(RSTT, [KD, NT * P])
        rst_t = at(RSTT, [KD, NT * P])
        k_hl = [split_tensor(f"k_hl{i}", b, [N]) for i, b in enumerate((SET0, SET1))]
        q_hi = [split_tensor(f"q_hi{i}", b + 4 * N, [N]) for i, b in enumerate((SET0, SET1))]
        q_lo = [split_tensor(f"q_lo{i}", b + 8 * N, [N]) for i, b in enumerate((SET0, SET1))]
        k_lo = split_tensor("k_lo", TMPK, [N])
        p_hi = split_tensor("p_hi", PROBS, [NPB, BW])
        p_lo = split_tensor("p_lo", PROBS + NPB * 4 * BW, [NPB, BW])
        rst = at(RSTB, [D])
        spare = at(SPAREB, [OHW // 2], parts=CE).bitcast(f16)
        q_t = at(QT, [PAIRS, N])
        k_t = at(KT, [PAIRS, NT * P])
        v_hl = split_tensor("v_hl", VT, [NT, HEADS, 2, DH])
        w_qkv = at(SET1, [KD, 3 * D])
        w1 = at(SET0, [KD, HID])
        w2 = at(SET1, [KH, D])
        w_o = at(SET1 + KH * D * 4, [KD, D])
        h_t = at(KT, [KH, N])
        xr = at(VT + NT * D * 4, [NT, D])
        E_BASE = 16384 // 4
        b1_all = at(0, [EXP * DFF])
        x2n = at(57344, [NT, D])
        x2n_t = at(77824, [2, KD, P])
        R0 = 81920

        def small(k, *shape):
            return at(R0 + 640 * k, list(shape))

        logits, prob, tmp, oh1, oh2, rank, gates = (small(k, NT, EXP) for k in range(7))
        tcmp = at(R0, [MAXT, EXP])
        cum = at(R0, [EXP, EXP])
        total = at(R0 + 4480, [EXP])
        ntile = at(R0 + 4544, [EXP])
        tstart = at(R0 + 4608, [EXP])
        tend = at(R0 + 4672, [EXP])
        red, red2, red3, sums_red = (at(R0 + 4736 + 40 * k, [NT]) for k in range(4))
        tef = at(R0 + 4896, [MAXT])
        many = at(R0 + 5056, [EXP, NT])
        S = 147456
        xg = at(S, [2, D])
        xg_t = at(S + 4096, [2, KD, P])
        hb = at(S + 8192, [2, DFF])
        hg = at(S + 10240, [2, DFF])
        hg_t = at(S + 12288, [2, KF, P])
        y_sb = at(S + 14336, [2, D])
        gates_t = at(S + 18432, [NT * P], parts=EXP)
        yg = at(0, [2, NT, D])

        ident = sb("ident", [P, P])
        spare_col = sb("spare_col", [CE, 2, 1])
        bias_b2, bias_bo = sb("bias_b2", [P, D]), sb("bias_bo", [P, D])
        iota16 = sb("iota16", [P, WCOL], f16)
        tri = sb("tri", [P, P], bf16)
        ones = sb("ones", [P, P], bf16)
        mask16 = sb("mask16", [P, NT * EXP], bf16)
        win_idx = sb("win_idx", [CP, NW])
        chunk_idx = sb("chunk_idx", [CP, CJ])
        chunk_neg = sb("chunk_neg", [CP, CJ])
        first5 = sb("first5", [CP, CJ])
        last5 = sb("last5", [CP, CJ])
        mincol = sb("mincol", [CP, 1])
        minrow = sb("minrow", [1, 2 * NW])
        bounds = sb("bounds", [1, NW, 2], i32)
        valid = sb("valid", [P, NT])
        einv = sb("einv", [P, EXP])
        thr = sb("thr", [P, NT])
        tidx = sb("tidx", [P, MAXT])
        below = sb("below", [P, EXP, EXP])
        eps_c = sb("eps_c", [P, 1])
        eps1 = sb("eps1", [P, 1])
        b1 = sb("b1", [P, KH])
        rw_sb = sb("rw_sb", [P, KD, EXP])
        rb_sb = sb("rb_sb", [P, EXP])
        b2_sb = sb("b2_sb", [EXP, D])
        stats = sb("stats", [P, NT, 6])
        mv = sb("mv", [P, NT, 2])
        std = sb("std", [P, NT])
        rstd = sb("rstd", [P, NT])
        gate = sb("gate", [P, 2, NT])
        slot = sb("slot", [P, 2, NT], i32)
        te = sb("te", [P, MAXT], i32)
        npair = sb("npair", [P, 1], i32)

        bank = [ctx.enter_context(nc.psum_tensor(f"bank{i}", [P, 512], f32)) for i in range(8)]
        NQB, AV, AW, NB = 3, 3, (5, 7), 6

        x_in = [sem(f"x_in{i}") for i in range(3)]
        edges_in, bias_in, b1_in, rw_in, rb_in, b2_in, eps_in = (
            sem(s) for s in ("edges_in", "bias_in", "b1_in", "rw_in", "rb_in", "b2_in", "eps_in"))
        x_again = sem("x_again")
        wqkv_in, w1_in, w2_in, wo_in, eb1_in = (sem(s) for s in ("wqkv_in", "w1_in", "w2_in", "wo_in", "eb1_in"))
        ew_in = [sem(f"ew_in{e}") for e in range(EXP)]
        zero_filled = sem("zero_filled")
        xpad_ready, zeros_ready, pool_chain, consts_ready = (
            sem(s) for s in ("xpad_ready", "zeros_ready", "pool_chain", "consts_ready"))
        base_ready = sem("base_ready")
        dve_chain, var_ready, std_ready, xn_ready = (sem(s) for s in ("dve_chain", "var_ready", "std_ready", "xn_ready"))
        xnt_ps, xnt_saved = sem("xnt_ps"), sem("xnt_saved")
        proj_ps, proj_saved = sem("proj_ps"), sem("proj_saved")
        edge_ready, edge_ps, edge_saved, min_ps = (sem(s) for s in ("edge_ready", "edge_ps", "edge_saved", "min_ps"))
        marks_ready, mins_ps, mincol_ready, bounds_ready = (
            sem(s) for s in ("marks_ready", "mins_ps", "mincol_ready", "bounds_ready"))
        onehots_ready, onehots_used = sem("onehots_ready"), sem("onehots_used")
        spare_ready, spare_used = sem("spare_ready"), sem("spare_used")
        spare_chain, spare_waited = sem("spare_chain"), sem("spare_waited")
        chunks_ready, cols_ready = sem("chunks_ready"), sem("cols_ready")
        window_saved = sem("window_saved")
        neigh_ps, rst_ready, rstt_ps, rstt_saved = (sem(s) for s in ("neigh_ps", "rst_ready", "rstt_ps", "rstt_saved"))
        qk_ps, p_hi_ready, p_lo_ready, av_step, av_half, av_saved = (
            sem(s) for s in ("qk_ps", "p_hi_ready", "p_lo_ready", "av_step", "av_half", "av_saved"))
        v_hi_ready, v_lo_ready = sem("v_hi_ready"), sem("v_lo_ready")
        head_split = sem("head_split")
        head_ready = [sem(f"head_ready{h}") for h in range(HEADS)]
        hid_ps, hid_saved = sem("hid_ps"), sem("hid_saved")
        mix_ps, x2_ready = sem("mix_ps"), sem("x2_ready")
        var2_ready, std2_ready, x2n_ready, x2nt_ps, x2nt_saved, logit_ps = (
            sem(s) for s in ("var2_ready", "std2_ready", "x2n_ready", "x2nt_ps", "x2nt_saved", "logit_ps"))
        shifted_ready, exp_ready, mask_ready, rank_ps, route_ready = (
            sem(s) for s in ("shifted_ready", "exp_ready", "mask_ready", "rank_ps", "route_ready"))
        gates_ready, gt_ps, gt_saved, gb_ps, gb_added = (
            sem(s) for s in ("gates_ready", "gt_ps", "gt_saved", "gb_ps", "gb_added"))
        scattered, w_ready = sem("scattered"), sem("w_ready")
        xg_in = [sem(f"xg_in{i}") for i in range(2)]
        xgt_ps = [sem(f"xgt_ps{i}") for i in range(2)]
        xgt_saved = [sem(f"xgt_saved{i}") for i in range(2)]
        h_ps = [sem(f"h_ps{i}") for i in range(2)]
        hb_ready = [sem(f"hb_ready{i}") for i in range(2)]
        hg_ready = [sem(f"hg_ready{i}") for i in range(2)]
        hgt_ps = [sem(f"hgt_ps{i}") for i in range(2)]
        hgt_saved = [sem(f"hgt_saved{i}") for i in range(2)]
        y_ps = [sem(f"y_ps{i}") for i in range(2)]
        y_saved = [sem(f"y_saved{i}") for i in range(2)]
        y_stored = [sem(f"y_stored{i}") for i in range(2)]
        yg_in = [sem(f"yg_in{t}") for t in range(NT)]
        rows_stored, res_ready, stored = sem("rows_stored"), sem("res_ready"), sem("stored")

        def rows(t):
            return LAST if t == NT - 1 else P

        projections = [(which, p, b) for p in range(PAIRS) for which in ("k", "q") for b in range(len(BLOCKS))]
        NPROJ = len(projections)
        steps = [(h, b, t) for h in range(HEADS) for b in range(len(BLOCKS)) for t in range(NT)]
        NS = len(steps)
        SPH = len(BLOCKS) * NT
        EVERY = 5.4
        pe_after, act_after, dve_after = ([[] for _ in range(NS)] for _ in range(3))
        for w in range(NW):
            for k in range(USUAL[w]):
                made = int(w * EVERY + k * EVERY / USUAL[w])
                dve_after[made].append(("pair", w, k))
                pe_after[made + 1].append(("pair", w, k))
            act_after[made + 4].append(("window", w))
            if w % WPG == WPG - 1:
                g = w // WPG
                for t in range(NT):
                    pe_after[made + 5 + t].append(("sum", g, t))
                dve_after[made + NT + 6].append(("sum", g))
                pe_after[made + NT + 7].append(("turn", g))
                act_after[made + NT + 10].append(("turn", g))

        block = ctx.enter_context(nc.Block())

        @block.sync
        def _(sp):
            xv = x[0:(NT - 1) * P, :].rearrange("(t p) d -> p t d", p=P)
            sp.dma_start(xr[:, 0:5, :], xv[:, 0:5, :]).then_inc(x_in[0], 16)
            sp.dma_start(xr[:, 5:9, :], xv[:, 5:9, :]).then_inc(x_in[1], 16)
            sp.wait_ge(xpad_ready, 1)
            sp.dma_start(xr[0:LAST, NT - 1, :], x[(NT - 1) * P:N, :]).then_inc(x_in[2], 16)
            for k in range(KD):
                sp.dma_start(w_qkv[:, k, :], wqkv[:, k, :]).then_inc(wqkv_in, 16)
            sp.wait_ge(zeros_ready, 1)
            sp.dma_start(xs.rearrange("(t p) d -> p t d", p=P),
                         zeros.unsqueeze(1).to_broadcast([P, MAXT, D])).then_inc(zero_filled, 16)
            for h in range(HEADS):
                own, other = slice(DH * (h % 2), DH * (h % 2) + DH), slice(DH - DH * (h % 2), 2 * DH - DH * (h % 2))
                sp.wait_ge(head_split, h + 1)
                for to, of in ((k_hl[h % 2], k_lo), (q_hi[h % 2], q_hi[h % 2]), (q_lo[h % 2], q_lo[h % 2])):
                    sp.dma_start(to[other, :].bitcast(f32), of[own, :].bitcast(f32)).then_inc(head_ready[h], 16)
            sp.wait_ge(qk_ps, SPH * (HEADS - 1))
            sp.wait_ge(head_ready[HEADS - 1], 48)
            sp.dma_start(w1[:, :, :], gw1).then_inc(w1_in, 16)

            def expert(e):
                sp.dma_start(arena[:, E_BASE + e * EW:E_BASE + (e + 1) * EW], ew[e]).then_inc(ew_in[e], 16)

            sp.wait_ge(rstt_ps, NT)
            sp.wait_ge(av_step, NS)
            sp.dma_start(xr[:, 0:9, :], xv).then_inc(x_again, 16)
            sp.wait_ge(xpad_ready, 2)
            sp.dma_start(xr[0:LAST, NT - 1, :], x[(NT - 1) * P:N, :]).then_inc(x_again, 16)
            sp.dma_start(w2[:, :, :], gw2).then_inc(w2_in, 16)
            sp.dma_start(w_o[:, :, :], wo).then_inc(wo_in, 16)
            sp.dma_start(b1_all, eb1.partition_broadcast(P)).then_inc(eb1_in, 16)
            expert(0)
            sp.wait_ge(base_ready, NT)
            for e in (1, 2):
                expert(e)
            sp.wait_ge(hid_ps, KH * 3)
            for e in (3, 4):
                expert(e)
            sp.wait_ge(mix_ps, NT)
            for e in range(9, EXP):
                expert(e)
            sp.wait_ge(scattered, 16 * 2 * NT)
            sp.wait_ge(zero_filled, 16)
            for a in range(2):
                sp.dma_start(xg[:, a, :], xs[a * P:(a + 1) * P, :]).then_inc(xg_in[a], 16)
            n = sp.value_load(npair[0:1, 0:1], min_val=1, max_val=(MAXT - 1) // 2)
            with sp.Fori(0, n) as j:
                for a in range(2):
                    sp.wait_ge(xgt_ps[a], j + 1)
                    sp.dma_start(xg[:, a, :], xs[bass.ds((2 * j + 2 + a) * P, P), :]).then_inc(xg_in[a], 16)
                for a in range(2):
                    sp.wait_ge(y_saved[a], j + 2)
                    sp.dma_start(xs[bass.ds((2 * j + a) * P, P), :], y_sb[:, a, :]).then_inc(y_stored[a], 16)
            for a in range(2):
                sp.wait_ge(xg_in[a], 16 * (n + 1))
            for t in range(NT):
                sp.wait_ge(res_ready, t + 1)
                sp.dma_start(out[t * P:t * P + rows(t), :], xr[0:rows(t), t, :]).then_inc(stored, 16)
            sp.wait_ge(stored, 16 * NT)

        @block.gpsimd
        def _(pool):
            count = [0]

            def link(ins):
                count[0] += 1
                ins.then_inc(pool_chain, 1)
                pool.wait_ge(pool_chain, count[0])

            link(pool.memset(xr[96:P, NT - 1, :], 0.0))
            pool.sem_inc(xpad_ready, 1)
            pool.dma_start(dst_i, dst.rearrange("(p n) -> p n", p=CP)).then_inc(edges_in, 16)
            pool.dma_start(src_i, src.rearrange("(p n) -> p n", p=CP)).then_inc(edges_in, 16)
            pool.dma_start(bias_b2[:, :], gb2.partition_broadcast(P)).then_inc(bias_in, 16)
            pool.dma_start(bias_bo[:, :], bo.partition_broadcast(P)).then_inc(bias_in, 16)
            pool.dma_start(b1[:, :], gb1).then_inc(b1_in, 16)
            pool.dma_start(rw_sb[:, :, :], rw).then_inc(rw_in, 16)
            pool.dma_start(rb_sb[:, :], rb.partition_broadcast(P)).then_inc(rb_in, 16)
            pool.dma_start(eps_c[:, :], geps.partition_broadcast(P)).then_inc(eps_in, 16)
            pool.dma_start(b2_sb[:, :], eb2).then_inc(b2_in, 16)
            link(pool.memset(ident[:, :], 0.0))
            link(pool.affine_select(out=ident[:, :], in_=ident[:, :], compare_op=ALU.not_equal, fill=1.0,
                                    base=0, pattern=[[-1, P]], channel_multiplier=1))
            pool.sem_inc(consts_ready, 1)
            link(pool.memset(zeros, 0.0))
            pool.sem_inc(zeros_ready, 1)
            link(pool.memset(tri[:, :], 1.0))
            link(pool.affine_select(out=tri[:, :], in_=tri[:, :], compare_op=ALU.is_ge, fill=0.0,
                                    base=-1, pattern=[[1, P]], channel_multiplier=-1))
            link(pool.memset(valid[:, :], 1.0))
            link(pool.affine_select(out=valid[:, NT - 1:NT], in_=valid[:, NT - 1:NT], compare_op=ALU.is_ge,
                                    fill=0.0, base=LAST - 1, pattern=[[0, 1]], channel_multiplier=-1))
            link(pool.memset(below[:, :, :], 1.0))
            link(pool.affine_select(out=below[:, :, :], in_=below[:, :, :], compare_op=ALU.is_ge, fill=0.0,
                                    base=-1, pattern=[[1, EXP], [-1, EXP]], channel_multiplier=0))
            link(pool.memset(ones[:, :], 1.0))

            def ramp(t, pattern, base=0, per_partition=0):
                link(pool.iota(t, pattern=pattern, base=base, channel_multiplier=per_partition,
                               allow_small_or_imprecise_dtypes=True))

            ramp(iota16[:, :], [[1, WCOL]])
            ramp(win_idx[:, :], [[1, NW]])
            ramp(chunk_idx[:, :], [[1, CJ]], 0, CJ)
            ramp(chunk_neg[:, :], [[-1, CJ]], 0, -CJ)
            ramp(einv[:, :], [[-1, EXP]], EXP)
            ramp(thr[:, :], [[P, NT]])
            ramp(tidx[:, :], [[1, MAXT]])
            pool.sem_inc(consts_ready, 1)
            pool.wait_ge(bias_in, 32)
            link(pool.tensor_tensor(bias_b2[:, :], bias_b2[:, :], bias_bo[:, :], ALU.add))
            def split_head(h):
                p, own, i = h // 2, slice(DH * (h % 2), DH * (h % 2) + DH), h % 2
                pool.wait_ge(proj_saved, 6 * (p + 1))
                if h >= 1:
                    pool.wait_ge(head_ready[h - 1], 48)
                if h >= 2:
                    pool.wait_ge(qk_ps, SPH * (h - 1))
                if h == 1:
                    pool.wait_ge(proj_ps, NPROJ + NT)
                link(pool.tensor_copy(k_hl[i][own, :], k_t[own, p, 0:N]))
                link(pool.tensor_tensor(k_lo[own, :], k_t[own, p, 0:N], k_hl[i][own, :].bitcast(f32), ALU.subtract))
                link(pool.tensor_copy(q_hi[i][own, :], q_t[own, p, :]))
                link(pool.tensor_tensor(q_lo[i][own, :], q_t[own, p, :], q_hi[i][own, :].bitcast(f32), ALU.subtract))
                pool.sem_inc(head_split, 1)

            def window_columns(w):
                if w == 0:
                    pool.wait_ge(chunks_ready, 1)
                if w >= WBUF:
                    pool.wait_ge(onehots_ready, FIRST[w - WBUF + 1])
                n = USUAL[w]
                lo = pool.value_load(bounds[0:1, w, 0:1], min_val=0, max_val=NC - 1)
                to = window_cols[:, w % WBUF, :, 0:n]
                link(pool.tensor_copy(to, edge_cols[:, :, bass.ds(lo, n)]))
                link(pool.tensor_scalar(to[:, 0, :], to[:, 0, :], float(-WCOL * w), None, ALU.add))
                pool.sem_inc(cols_ready, 1)

            pairs, links, chunk = (pool.alloc_register(f"pool_{s}") for s in ("pairs", "links", "chunk"))
            pool.reg_mov(pairs, 0)
            pool.reg_mov(links, 0)

            def link_spare(ins):
                ins.then_inc(spare_chain, 1)
                pool.reg_add(links, links, 1)
                pool.wait_ge(spare_chain, pool.snap(links, min_val=1, max_val=2 * NW * NC))
                pool.sem_inc(spare_waited, 1)

            def spare_chunks(w):
                extra = pool.value_load(bounds[0:1, w, 1:2], min_val=0, max_val=NC)
                with pool.If(extra > 0):
                    lo = pool.value_load(bounds[0:1, w, 0:1], min_val=0, max_val=NC - 1)
                    pool.reg_mov(chunk, lo + USUAL[w])
                    with pool.Fori(0, extra):
                        pool.wait_ge(spare_used, pool.snap(pairs, min_val=0, max_val=NW * NC) + 1)
                        pool.sem_inc(spare_waited, 1)
                        link_spare(pool.tensor_copy(
                            spare_col[:, :, :], edge_cols[:, :, bass.ds(pool.snap(chunk, min_val=0, max_val=NC - 1), 1)]))
                        link_spare(pool.tensor_scalar(spare_col[:, 0, :], spare_col[:, 0, :], float(-WCOL * w), None,
                                                      ALU.add))
                        pool.tensor_scalar(spare[:, 0:P], iota16[0:CE, 0:P], spare_col[:, 1, :], None, ALU.is_equal)
                        pool.tensor_scalar(spare[:, P:OHW], iota16[0:CE, :], spare_col[:, 0, :], None,
                                           ALU.is_equal).then_inc(spare_ready, 1)
                        pool.reg_add(pairs, pairs, 1)
                        pool.reg_add(chunk, chunk, 1)
                    pool.wait_ge(spare_ready, pool.snap(pairs, min_val=1, max_val=NW * NC))
                    pool.sem_inc(spare_waited, 1)

            for _, what, i in sorted([(SPH * (h - 1) + 1, "head", h) for h in range(HEADS)]
                                     + [(int((w - 2) * EVERY), "cols", w) for w in range(NW)]
                                     + [(int(w * EVERY), "spare", w) for w in range(NW)]):
                {"head": split_head, "cols": window_columns, "spare": spare_chunks}[what](i)
            pool.wait_ge(av_step, NS)
            link(pool.memset(xr[96:P, NT - 1, :], 0.0))
            pool.sem_inc(xpad_ready, 1)
            pool.wait_ge(x_again, 32)
            for t in range(NT):
                link(pool.tensor_tensor(xr[:, t, :], xr[:, t, :], xn[:, t, :], ALU.add))
                link(pool.tensor_tensor(xr[:, t, :], xr[:, t, :], bias_b2[:, :], ALU.add))
                pool.sem_inc(base_ready, 1)
            pool.wait_ge(route_ready, 1)
            pool.wait_ge(zero_filled, 16)
            for t in range(NT):
                for k in range(2):
                    pool.indirect_dma_start(
                        out=xs, out_offset=bass.IndirectOffsetOnAxis(ap=slot[0:rows(t), k, t:t + 1], axis=0),
                        in_=x2n[0:rows(t), t, :], in_offset=None).then_inc(scattered, 16)
            for e in range(EXP):
                pool.wait_ge(ew_in[e], 16)
                pool.sem_inc(w_ready, 1)
            n = pool.value_load(npair[0:1, 0:1], min_val=1, max_val=(MAXT - 1) // 2)
            for a in range(2):
                pool.wait_ge(y_stored[a], 16 * n + 16)
                pool.sem_inc(rows_stored, 1)
            pool.wait_ge(rows_stored, 2)
            for t in range(NT):
                for k in range(2):
                    pool.indirect_dma_start(
                        out=yg[0:rows(t), k, t, :], out_offset=None, in_=xs,
                        in_offset=bass.IndirectOffsetOnAxis(ap=slot[0:rows(t), k, t:t + 1], axis=0)
                    ).then_inc(yg_in[t], 16)

        @block.scalar
        def _(act):
            copy = ACT.Copy
            for half in range(2):
                act.wait_ge(var_ready, half + 1)
                act.activation(std[:, 5 * half:5 * half + 5], std[:, 5 * half:5 * half + 5],
                               ACT.Sqrt).then_inc(std_ready, 1)
            for t in range(NT):
                act.wait_ge(xnt_ps, t + 1)
                act.activation(xn_t[:, :, t * P:(t + 1) * P],
                               bank[6 + t % 2][:, :].rearrange("p (k n) -> p k n", k=KD),
                               copy).then_inc(xnt_saved, 1)
            for g, (which, p, b) in enumerate(projections):
                o, n = BLOCKS[b]
                act.wait_ge(proj_ps, g + 1)
                if which == "k":
                    act.activation(k_t[:, p, o:o + n], bank[g % 5][:, 0:n], copy).then_inc(proj_saved, 1)
                else:
                    act.activation(q_t[:, p, o:o + n], bank[g % 5][:, 0:n], copy, scale=SCALE).then_inc(proj_saved, 1)
            for t in range(NT):
                act.wait_ge(proj_ps, NPROJ + t + 1)
                act.activation(v_hl[:, t, :, 0, :], bank[(NPROJ + t) % 5][:, :].rearrange("p (h d) -> p h d", h=HEADS),
                               copy).then_inc(v_hi_ready, 1)

            def save_attention(m):
                h, b = m // 3, m % 3
                o, n = BLOCKS[b]
                act.wait_ge(av_step, NT * (m + 1))
                act.activation(q_t[DH * (h % 2):DH * (h % 2) + DH, h // 2, o:o + n], bank[AV + m % 2][0:DH, 0:n],
                               copy).then_inc(av_half, 1)

            for s, (h, b, t) in enumerate(steps):
                n = BLOCKS[b][1]
                kt = rows(t)
                act.wait_ge(qk_ps, s + 1)
                if s >= NPB:
                    act.wait_ge(av_step, s - NPB + 1)
                if s == 0:
                    act.wait_ge(proj_ps, NPROJ + NT)
                act.activation(p_hi[0:kt, s % NPB, 0:n], bank[s % NQB][0:kt, 0:n], ACT.Relu).then_inc(p_hi_ready, 1)
                if s > NT and s % NT == 1:
                    save_attention(s // NT - 1)
                for what, i in act_after[s]:
                    if what == "window":
                        act.wait_ge(onehots_used, FIRST[i + 1])
                        g = i // WPG
                        if i % WPG == 0 and g >= 2:
                            act.wait_ge(neigh_ps, g - 1)
                        if i == 0:
                            act.wait_ge(zero_filled, 16)
                        act.activation(a_t[:, g % 2, :, (i % WPG) * WD:(i % WPG + 1) * WD],
                                       bank[AW[i % 2]][:, 0:WCOL].rearrange("p (b d) -> p b d", b=NT),
                                       copy).then_inc(window_saved, 1)
                    else:
                        act.wait_ge(rstt_ps, i + 1)
                        act.activation(rst_t[:, :, i * P:(i + 1) * P],
                                       bank[NB][:, :].rearrange("p (k n) -> p k n", k=KD), copy).then_inc(rstt_saved, 1)
            save_attention(HEADS * 3 - 1)
            act.wait_ge(b1_in, 16)
            g = 0
            for m in range(KH):
                for o, n in BLOCKS:
                    act.wait_ge(hid_ps, g + 1)
                    act.activation(h_t[:, m, o:o + n], bank[g % 4][:, 0:n], ACT.Relu,
                                   bias=b1[:, m:m + 1]).then_inc(hid_saved, 1)
                    g += 1
            for t in range(NT):
                act.wait_ge(var2_ready, t + 1)
                act.activation(std[:, t:t + 1], std[:, t:t + 1], ACT.Sqrt).then_inc(std2_ready, 1)
                act.wait_ge(x2nt_ps, t + 1)
                if t >= 2:
                    act.wait_ge(logit_ps, t - 1)
                act.activation(x2n_t[:, t % 2, :, :], bank[6][:, :].rearrange("p (k n) -> p k n", k=KD),
                               copy).then_inc(x2nt_saved, 1)
            act.wait_ge(shifted_ready, 1)
            act.activation(prob[:, :, :], logits[:, :, :], ACT.Exp).then_inc(exp_ready, 1)
            for t in range(NT):
                act.wait_ge(gt_ps, t + 1)
                act.activation(gates_t[:, t * P:(t + 1) * P], bank[t % 2][0:EXP, 0:P], copy).then_inc(gt_saved, 1)
            act.wait_ge(scattered, 16 * 2 * NT)
            for e in range(5, 9):
                act.dma_start(arena[:, E_BASE + e * EW:E_BASE + (e + 1) * EW], ew[e]).then_inc(ew_in[e], 16)
            for a in range(2):
                act.wait_ge(xgt_ps[a], 1)
                act.activation(xg_t[:, a, :, :], bank[4 + a][:, :].rearrange("p (k n) -> p k n", k=KD),
                               copy).then_inc(xgt_saved[a], 1)
            n = act.value_load(npair[0:1, 0:1], min_val=1, max_val=(MAXT - 1) // 2)
            with act.Fori(0, n) as j:
                for a in range(2):
                    act.wait_ge(hb_ready[a], j + 2)
                    act.activation(hg[:, a, :], hb[:, a, :], ACT.Gelu).then_inc(hg_ready[a], 1)
                for a in range(2):
                    act.wait_ge(xgt_ps[a], j + 2)
                    act.activation(xg_t[:, a, :, :], bank[4 + a][:, :].rearrange("p (k n) -> p k n", k=KD),
                                   copy).then_inc(xgt_saved[a], 1)

        @block.vector
        def _(dve):
            count = [0]

            def link(ins):
                count[0] += 1
                ins.then_inc(dve_chain, 1)
                dve.wait_ge(dve_chain, count[0])

            for half in range(2):
                for t in range(5 * half, 5 * half + 5):
                    if t == 0:
                        dve.wait_ge(x_in[0], 16)
                    if t == 5:
                        dve.wait_ge(x_in[1], 16)
                    if t == NT - 1:
                        dve.wait_ge(x_in[2], 16)
                        dve.wait_ge(xpad_ready, 1)
                    ins = dve.bn_stats(stats[:, t, :], xr[:, t, :])
                link(ins)
                for t in range(5 * half, 5 * half + 5):
                    ins = dve.bn_aggr(mv[:, t, :], stats[:, t, :])
                link(ins)
                dve.tensor_scalar_add(std[:, 5 * half:5 * half + 5], mv[:, 5 * half:5 * half + 5, 1],
                                      EPS).then_inc(var_ready, 1)
                dve.wait_ge(std_ready, half + 1)
                link(dve.reciprocal(rstd[:, 5 * half:5 * half + 5], std[:, 5 * half:5 * half + 5]))
                for t in range(5 * half, 5 * half + 5):
                    dve.tensor_scalar(xn[:, t, :], xr[:, t, :], mv[:, t, 0:1], rstd[:, t:t + 1],
                                      ALU.subtract, ALU.mult).then_inc(xn_ready, 1)
            dve.wait_ge(edges_in, 32)
            dve.wait_ge(consts_ready, 2)
            dve.tensor_single_scalar(win_i, dst_i, 5, op=ALU.arith_shift_right)
            dve.tensor_single_scalar(off_i, dst_i, WD - 1, op=ALU.bitwise_and)
            dve.tensor_single_scalar(hi_i, src_i, 7, op=ALU.arith_shift_right)
            link(dve.tensor_single_scalar(lo_i, src_i, P - 1, op=ALU.bitwise_and))
            dve.tensor_copy(lo_f, lo_i).then_inc(edge_ready, 1)
            win_v = win_i.rearrange("p (j n) -> p j n", j=CJ)
            dve.tensor_reduce(first5[:, :], win_v, X, ALU.min)
            dve.tensor_reduce(last5[:, :], win_v, X, ALU.max)
            link(dve.scalar_tensor_tensor(out=val_f, in0=win_i, scalar=float(NT), in1=hi_i,
                                          op0=ALU.mult, op1=ALU.add))
            dve.scalar_tensor_tensor(out=val_f, in0=val_f, scalar=float(WD), in1=off_i,
                                     op0=ALU.mult, op1=ALU.add).then_inc(edge_ready, 1)
            for jj in range(CJ):
                dve.tensor_scalar(marks[:, 0, :, jj], win_idx[:, :], last5[:, jj:jj + 1], FAR, ALU.is_gt, ALU.mult)
                last = dve.tensor_scalar(marks[:, 1, :, jj], win_idx[:, :], first5[:, jj:jj + 1], FAR,
                                         ALU.is_lt, ALU.mult)
            link(last)
            for jj in range(CJ):
                dve.tensor_scalar(marks[:, 0, :, jj], marks[:, 0, :, jj], chunk_idx[:, jj:jj + 1], None, ALU.add)
                last = dve.tensor_scalar(marks[:, 1, :, jj], marks[:, 1, :, jj], chunk_neg[:, jj:jj + 1], None,
                                         ALU.add)
            link(last)
            dve.tensor_reduce(marks2, marks.rearrange("p a w j -> p (a w) j"), X, ALU.min).then_inc(marks_ready, 1)
            dve.wait_ge(mins_ps, 1)
            dve.tensor_reduce(mincol[:, :], bank[AW[0]][0:2 * NW, 0:CP], X, ALU.min).then_inc(mincol_ready, 1)
            dve.wait_ge(min_ps, 1)
            link(dve.tensor_copy(minrow[:, :], bank[NB][0:1, 0:2 * NW]))
            link(dve.tensor_scalar(minrow[:, 0:NW], minrow[:, 0:NW], float(NC - 1), None, ALU.min))
            link(dve.tensor_scalar(minrow[:, NW:2 * NW], minrow[:, NW:2 * NW], -1.0, None, ALU.mult))
            link(dve.tensor_tensor(minrow[:, NW:2 * NW], minrow[:, NW:2 * NW], minrow[:, 0:NW], ALU.max))
            link(dve.tensor_tensor(minrow[:, NW:2 * NW], minrow[:, NW:2 * NW], minrow[:, 0:NW], ALU.subtract))
            for of, usual in ((minrow[:, NW:2 * NW - 1], USUAL[0]), (minrow[:, 2 * NW - 1:2 * NW], USUAL[NW - 1])):
                last = dve.tensor_scalar(of, of, float(1 - usual), 0.0, ALU.add, ALU.max)
            link(last)
            dve.tensor_copy(bounds[:, :, 0], minrow[:, 0:NW])
            dve.tensor_copy(bounds[:, :, 1], minrow[:, NW:2 * NW]).then_inc(bounds_ready, 1)
            dve.wait_ge(edge_ps, 1)
            dve.tensor_copy(low[:, 0:NC].rearrange("p (c j) -> p j c", j=CJ),
                            bank[AW[0]][0:CE, 0:NC].rearrange("p (j c) -> p j c", j=CJ)).then_inc(edge_saved, 1)
            dve.wait_ge(edge_ps, 2)
            link(dve.tensor_copy(val[:, 0:NC].rearrange("p (c j) -> p j c", j=CJ),
                                 bank[NB][0:CE, 0:NC].rearrange("p (j c) -> p j c", j=CJ)))
            dve.sem_inc(edge_saved, 1)

            dve.wait_ge(eps_in, 16)
            link(dve.tensor_scalar_add(eps1[:, :], eps_c[:, :], 1.0))
            dve.memset(val[:, NC:NCP], -1e6)
            link(dve.memset(low[:, NC:NCP], 0.0))
            dve.wait_ge(bounds_ready, 1)
            dve.sem_inc(chunks_ready, 1)
            for t in range(NT):
                dve.wait_ge(v_hi_ready, t + 1)
                dve.tensor_tensor(v_hl[:, t, :, 1, :], bank[(NPROJ + t) % 5][:, :].rearrange("p (h d) -> p h d", h=HEADS),
                                  v_hl[:, t, :, 0, :].bitcast(f32), ALU.subtract).then_inc(v_lo_ready, 1)

            def do(what, i, k=0):
                if what == "pair":
                    if k == 0:
                        dve.wait_ge(cols_ready, i + 1)
                    q = FIRST[i] + k
                    if q >= RING:
                        dve.wait_ge(onehots_used, q - RING + 1)
                    at_slot = (q % RING) * OHW
                    dve.tensor_scalar(ring[:, at_slot:at_slot + P], iota16[0:CE, 0:P],
                                      window_cols[:, i % WBUF, 1, k:k + 1], None, ALU.is_equal)
                    dve.tensor_scalar(ring[:, at_slot + P:at_slot + OHW], iota16[0:CE, :],
                                      window_cols[:, i % WBUF, 0, k:k + 1], None,
                                      ALU.is_equal).then_inc(onehots_ready, 1)
                else:
                    dve.wait_ge(neigh_ps, i + 1)
                    if i >= 1:
                        dve.wait_ge(rstt_ps, i)
                    dve.scalar_tensor_tensor(out=rst, in0=xn[:, i, :], scalar=eps1[:, 0:1], in1=bank[NB][:, :],
                                             op0=ALU.mult, op1=ALU.add).then_inc(rst_ready, 1)

            def add_attention(m):
                h, b = m // 3, m % 3
                o, n = BLOCKS[b]
                to = q_t[DH * (h % 2):DH * (h % 2) + DH, h // 2, o:o + n]
                dve.wait_ge(av_half, m + 1)
                dve.tensor_tensor(to, to, bank[AV + m % 2][DH:P, 0:n], ALU.add).then_inc(av_saved, 1)

            for s, (h, b, t) in enumerate(steps):
                n = BLOCKS[b][1]
                kt = rows(t)
                dve.wait_ge(p_hi_ready, s + 1)
                dve.scalar_tensor_tensor(out=p_lo[0:kt, s % NPB, 0:n], in0=bank[s % NQB][0:kt, 0:n], scalar=0.0,
                                         in1=p_hi[0:kt, s % NPB, 0:n].bitcast(f32), op0=ALU.max,
                                         op1=ALU.subtract).then_inc(p_lo_ready, 1)
                if s > NT and s % NT == 2:
                    add_attention(s // NT - 1)
                for what in dve_after[s]:
                    do(*what)
            add_attention(HEADS * 3 - 1)

            for t in range(NT):
                r = rows(t)
                if t == 0:
                    dve.wait_ge(base_ready, NT)
                dve.wait_ge(mix_ps, t + 1)
                link(dve.tensor_tensor(xr[0:r, t, :], xr[0:r, t, :], bank[4 + t % 2][0:r, :], ALU.add))
                dve.sem_inc(x2_ready, 1)
                link(dve.bn_stats(stats[:, t, :], xr[:, t, :]))
                link(dve.bn_aggr(mv[:, t, :], stats[:, t, :]))
                dve.tensor_scalar_add(std[:, t:t + 1], mv[:, t, 1:2], EPS).then_inc(var2_ready, 1)
                dve.wait_ge(std2_ready, t + 1)
                link(dve.reciprocal(rstd[:, t:t + 1], std[:, t:t + 1]))
                if t == 0:
                    dve.wait_ge(hid_ps, KH * 3)
                dve.tensor_scalar(x2n[:, t, :], xr[:, t, :], mv[:, t, 0:1], rstd[:, t:t + 1],
                                  ALU.subtract, ALU.mult).then_inc(x2n_ready, 1)

            def over_e(a):
                return a.unsqueeze(2).to_broadcast([P, NT, EXP])

            def over_t(a):
                return a.unsqueeze(1).to_broadcast([P, NT, EXP])

            dve.wait_ge(logit_ps, NT)
            dve.wait_ge(rb_in, 16)
            lg_ps = bank[7][:, 0:NT * EXP].rearrange("p (t e) -> p t e", e=EXP)
            link(dve.tensor_tensor(logits, lg_ps, over_t(rb_sb[:, :]), ALU.add))
            link(dve.tensor_reduce(red, logits, X, ALU.max))
            dve.tensor_tensor(logits, logits, over_e(red), ALU.subtract).then_inc(shifted_ready, 1)
            dve.wait_ge(exp_ready, 1)
            link(dve.tensor_reduce(red2, prob, X, ALU.add))
            link(dve.reciprocal(red3, red2))
            link(dve.tensor_tensor(prob, prob, over_e(red3), ALU.mult))
            for k, oh in ((0, oh1), (1, oh2)):
                link(dve.tensor_reduce(gate[:, k, :], prob, X, ALU.max))
                link(dve.tensor_tensor(tmp, prob, over_e(gate[:, k, :]), ALU.is_equal))
                link(dve.tensor_tensor(tmp, tmp, over_t(einv[:, :]), ALU.mult))
                link(dve.tensor_reduce(red, tmp, X, ALU.max))
                link(dve.tensor_tensor(oh, over_t(einv[:, :]), over_e(red), ALU.is_equal))
                if k == 0:
                    link(dve.scalar_tensor_tensor(out=prob, in0=oh1, scalar=-2.0, in1=prob,
                                                  op0=ALU.mult, op1=ALU.add))
            link(dve.tensor_tensor(tmp, oh1, oh2, ALU.add))
            mask_v = mask16[:, :].rearrange("p (t e) -> p t e", e=EXP)
            link(dve.tensor_tensor(mask_v, tmp, over_e(valid[:, :]), ALU.mult))
            dve.sem_inc(mask_ready, 1)
            dve.tensor_tensor(tmp, oh1, over_e(gate[:, 0, :]), ALU.mult)
            link(dve.tensor_tensor(gates, oh2, over_e(gate[:, 1, :]), ALU.mult))
            link(dve.tensor_tensor(gates, gates, tmp, ALU.add))
            dve.sem_inc(gates_ready, 1)
            dve.wait_ge(rank_ps, 1)
            link(dve.tensor_copy(total, bank[3][:, 0:EXP]))
            link(dve.tensor_tensor(many, total.unsqueeze(2).to_broadcast([P, EXP, NT]),
                                   thr[:, :].unsqueeze(1).to_broadcast([P, EXP, NT]), ALU.is_gt))
            link(dve.tensor_reduce(ntile, many, X, ALU.add))
            link(dve.tensor_tensor(cum, ntile.unsqueeze(1).to_broadcast([P, EXP, EXP]), below[:, :, :], ALU.mult))
            link(dve.tensor_reduce(tstart, cum, X, ALU.add))
            dve.tensor_tensor(tend, tstart, ntile, ALU.add)
            link(dve.tensor_scalar(total, tstart, float(P), None, ALU.mult))
            link(dve.tensor_tensor(rank, bank[2][:, 0:NT * EXP].rearrange("p (t e) -> p t e", e=EXP),
                                   over_t(total), ALU.add))
            for k, oh in ((0, oh1), (1, oh2)):
                link(dve.tensor_tensor(tmp, oh, rank, ALU.mult))
                s_k = (sums_red, red3)[k]
                link(dve.tensor_reduce(s_k, tmp, X, ALU.add))
                last = dve.tensor_copy(slot[:, k, :], s_k)
            link(last)
            link(dve.tensor_scalar(red2[:, 0:1], tend[:, EXP - 1:EXP], 1.0, None, ALU.add))
            link(dve.tensor_copy(npair[:, :], red2[:, 0:1]))
            link(dve.tensor_single_scalar(npair[:, :], npair[:, :], 1, op=ALU.arith_shift_right))
            link(dve.tensor_tensor(tcmp, tidx[:, :].unsqueeze(2).to_broadcast([P, MAXT, EXP]),
                                   tend.unsqueeze(1).to_broadcast([P, MAXT, EXP]), ALU.is_ge))
            link(dve.tensor_reduce(tef, tcmp, X, ALU.add))
            link(dve.tensor_scalar(te[:, :], tef, float(EXP - 1), None, ALU.min))
            dve.sem_inc(route_ready, 1)
            for t in range(NT):
                r = rows(t)
                dve.wait_ge(gb_ps, t + 1)
                dve.tensor_tensor(xr[0:r, t, :], xr[0:r, t, :], bank[2 + t % 2][0:r, :], ALU.add).then_inc(gb_added, 1)
            dve.wait_ge(eb1_in, 16)
            for a in range(2):
                dve.sem_inc(hb_ready[a], 1)
                dve.sem_inc(hgt_saved[a], 1)
                dve.sem_inc(y_saved[a], 1)
                dve.sem_inc(y_stored[a], 16)
            n = dve.value_load(npair[0:1, 0:1], min_val=1, max_val=(MAXT - 1) // 2)
            with dve.Fori(0, n) as j:
                for a in range(2):
                    e = dve.value_load(te[0:1, bass.ds(2 * j + a, 1)], min_val=0, max_val=EXP - 1)
                    dve.wait_ge(h_ps[a], j + 1)
                    dve.tensor_tensor(hb[:, a, :], bank[a][:, 0:DFF], b1_all[:, bass.ds(e * DFF, DFF)],
                                      ALU.add).then_inc(hb_ready[a], 1)
                for a in range(2):
                    dve.wait_ge(hgt_ps[a], j + 1)
                    dve.tensor_copy(hg_t[:, a, :, :],
                                    bank[2 + a][:, 0:KF * P].rearrange("p (k n) -> p k n", k=KF)
                                    ).then_inc(hgt_saved[a], 1)
                for a in range(2):
                    dve.wait_ge(y_ps[a], j + 1)
                    dve.wait_ge(y_stored[a], 16 * j + 16)
                    dve.tensor_copy(y_sb[:, a, :], bank[6 + a][:, :]).then_inc(y_saved[a], 1)
            for t in range(NT):
                r = rows(t)
                dve.wait_ge(yg_in[t], 32)
                link(dve.scalar_tensor_tensor(out=xr[0:r, t, :], in0=yg[0:r, 0, t, :], scalar=gate[0:r, 0, t:t + 1],
                                              in1=xr[0:r, t, :], op0=ALU.mult, op1=ALU.add))
                dve.scalar_tensor_tensor(out=xr[0:r, t, :], in0=yg[0:r, 1, t, :], scalar=gate[0:r, 1, t:t + 1],
                                         in1=xr[0:r, t, :], op0=ALU.mult, op1=ALU.add).then_inc(res_ready, 1)

        @block.tensor
        def _(pe):
            pe.sem_inc(spare_used, 1)
            pe.wait_ge(consts_ready, 2)
            for t in range(NT):
                pe.wait_ge(xn_ready, t + 1)
                if t >= 2:
                    pe.wait_ge(xnt_saved, t - 1)
                for k in range(KD):
                    ins = pe.transpose(bank[6 + t % 2][:, k * P:(k + 1) * P], xn[:, t, k * P:(k + 1) * P], ident[:, :])
                ins.then_inc(xnt_ps, 1)
            pe.wait_ge(xnt_saved, NT)
            pe.wait_ge(wqkv_in, 16 * KD)
            for g, (which, p, b) in enumerate(projections):
                o, n = BLOCKS[b]
                c = (D if which == "k" else 0) + p * P
                if g >= 5:
                    pe.wait_ge(proj_saved, g - 4)
                for k in range(KD):
                    ins = pe.matmul(bank[g % 5][:, 0:n], w_qkv[:, k, c:c + P], xn_t[:, k, o:o + n],
                                    start=(k == 0), stop=(k == KD - 1))
                ins.then_inc(proj_ps, 1)
            pe.wait_ge(proj_saved, NPROJ)
            pe.wait_ge(marks_ready, 1)
            pe.transpose(bank[AW[0]][0:2 * NW, 0:CP], marks2, ident[0:CP, 0:CP]).then_inc(mins_ps, 1)
            pe.wait_ge(mincol_ready, 1)
            pe.transpose(bank[NB][0:1, 0:CP], mincol[:, :], ident[0:CP, 0:CP]).then_inc(min_ps, 1)
            pe.wait_ge(bounds_ready, 1)
            pe.wait_ge(edge_ready, 2)
            for a, (bk, t) in enumerate(((AW[0], lo_f), (NB, val_f))):
                for jj in range(CJ):
                    ins = pe.transpose(bank[bk][0:CE, jj * CP:(jj + 1) * CP], t[:, jj * CE:(jj + 1) * CE],
                                       ident[0:CP, 0:CP])
                ins.then_inc(edge_ps, 1)
            pe.wait_ge(edge_saved, 2)
            for t in range(NT):
                if t >= 5:
                    pe.wait_ge(v_lo_ready, t - 4)
                for k in range(KD):
                    ins = pe.matmul(bank[(NPROJ + t) % 5][:, :], xn_t[:, k, t * P:(t + 1) * P], w_qkv[:, k, 2 * D:3 * D],
                                    start=(k == 0), stop=(k == KD - 1))
                ins.then_inc(proj_ps, 1)
            pe.wait_ge(v_lo_ready, NT)
            pairs = pe.alloc_register("pe_pairs")
            pe.reg_mov(pairs, 0)

            def count_pair(w, k):
                if k == 0 and w >= 2:
                    pe.wait_ge(window_saved, w - 1)

                def product(of, at_slot, start, stop):
                    return pe.matmul(bank[AW[w % 2]][:, 0:WCOL], of[:, at_slot:at_slot + P],
                                     of[:, at_slot + P:at_slot + OHW], start=start, stop=stop, skip_group_check=True)

                if k == USUAL[w] - 1:
                    extra = pe.value_load(bounds[0:1, w, 1:2], min_val=0, max_val=NC)
                    with pe.If(extra > 0):
                        with pe.Fori(0, extra):
                            pe.wait_ge(spare_ready, pe.snap(pairs, min_val=0, max_val=NW * NC) + 1)
                            product(spare, 0, False, False).then_inc(spare_used, 1)
                            pe.reg_add(pairs, pairs, 1)
                q = FIRST[w] + k
                pe.wait_ge(onehots_ready, q + 1)
                product(ring, (q % RING) * OHW, k == 0, k == USUAL[w] - 1).then_inc(onehots_used, 1)

            def neighbours(g, t):
                if t == 0:
                    pe.wait_ge(window_saved, WPG * (g + 1))
                    if g:
                        pe.wait_ge(rstt_saved, g)
                ins = pe.matmul(bank[NB][:, :], a_t[:, g % 2, t, :], xn[:, t, :], start=(t == 0), stop=(t == NT - 1))
                if t == NT - 1:
                    ins.then_inc(neigh_ps, 1)

            def turn(g):
                pe.wait_ge(rst_ready, g + 1)
                for k in range(KD):
                    ins = pe.transpose(bank[NB][:, k * P:(k + 1) * P], rst[:, k * P:(k + 1) * P], ident[:, :])
                ins.then_inc(rstt_ps, 1)

            def scores(s):
                h, b, t = steps[s]
                o, n = BLOCKS[b]
                kt = rows(t)
                if s >= NQB:
                    pe.wait_ge(p_lo_ready, s - NQB + 1)
                if s % SPH == 0:
                    pe.wait_ge(head_split, h + 1)
                    pe.wait_ge(head_ready[h], 48)
                for first, q in ((True, q_hi), (False, q_lo)):
                    ins = pe.matmul(bank[s % NQB][0:kt, 0:n], k_hl[h % 2][:, t * P:t * P + kt], q[h % 2][:, o:o + n],
                                    start=first, stop=not first)
                ins.then_inc(qk_ps, 1)

            scores(0)
            scores(1)
            for s, (h, b, t) in enumerate(steps):
                if s + 2 < NS:
                    scores(s + 2)
                n = BLOCKS[b][1]
                kt = rows(t)
                m = s // NT
                if t == 0 and m >= 2:
                    pe.wait_ge(av_saved, m - 1)
                pe.wait_ge(p_hi_ready, s + 1)
                pe.matmul(bank[AV + m % 2][:, 0:n], v_hl[0:kt, t, h, :, :], p_hi[0:kt, s % NPB, 0:n],
                          start=(t == 0), stop=False)
                pe.wait_ge(p_lo_ready, s + 1)
                pe.matmul(bank[AV + m % 2][:, 0:n], v_hl[0:kt, t, h, :, :], p_lo[0:kt, s % NPB, 0:n],
                          start=False, stop=(t == NT - 1)).then_inc(av_step, 1)
                for what in pe_after[s]:
                    {"pair": count_pair, "sum": neighbours, "turn": turn}[what[0]](*what[1:])

            pe.wait_ge(rstt_saved, NT)
            pe.wait_ge(w1_in, 16)
            g = 0
            for m in range(KH):
                for o, n in BLOCKS:
                    if g >= 4:
                        pe.wait_ge(hid_saved, g - 3)
                    for k in range(KD):
                        ins = pe.matmul(bank[g % 4][:, 0:n], w1[:, k, m * P:(m + 1) * P], rst_t[:, k, o:o + n],
                                        start=(k == 0), stop=(k == KD - 1))
                    ins.then_inc(hid_ps, 1)
                    g += 1

            def mix(t):
                r = rows(t)
                if t >= 2:
                    pe.wait_ge(x2_ready, t - 1)
                for m in range(KH):
                    pe.matmul(bank[4 + t % 2][0:r, :], h_t[:, m, t * P:t * P + r], w2[:, m, :], start=(m == 0), stop=False)
                for p in range(PAIRS):
                    ins = pe.matmul(bank[4 + t % 2][0:r, :], q_t[:, p, t * P:t * P + r], w_o[:, p, :],
                                    start=False, stop=(p == PAIRS - 1))
                ins.then_inc(mix_ps, 1)

            def turn_x2n(t):
                pe.wait_ge(x2n_ready, t + 1)
                if t:
                    pe.wait_ge(x2nt_saved, t)
                for k in range(KD):
                    ins = pe.transpose(bank[6][:, k * P:(k + 1) * P], x2n[:, t, k * P:(k + 1) * P], ident[:, :])
                ins.then_inc(x2nt_ps, 1)

            def route(t):
                pe.wait_ge(x2nt_saved, t + 1)
                for k in range(KD):
                    ins = pe.matmul(bank[7][:, t * EXP:(t + 1) * EXP], x2n_t[:, t % 2, k, :], rw_sb[:, k, :],
                                    start=(k == 0), stop=(k == KD - 1))
                ins.then_inc(logit_ps, 1)

            pe.wait_ge(hid_saved, g)
            pe.wait_ge(av_saved, HEADS * 3)
            pe.wait_ge(w2_in, 16)
            pe.wait_ge(wo_in, 16)
            pe.wait_ge(rw_in, 16)
            for t in range(NT + 2):
                if t < NT:
                    mix(t)
                if 0 <= t - 1 < NT:
                    turn_x2n(t - 1)
                if t >= 2:
                    route(t - 2)
            pe.wait_ge(mask_ready, 1)
            pe.matmul(bank[2][:, 0:NT * EXP], tri[:, :], mask16[:, :], start=True, stop=False, skip_group_check=True)
            for d in range(1, NT):
                pe.matmul(bank[2][:, d * EXP:NT * EXP], ones[:, :], mask16[:, 0:(NT - d) * EXP],
                          start=False, stop=(d == NT - 1), skip_group_check=True)
            for t in range(NT):
                ins = pe.matmul(bank[3][:, 0:EXP], ones[:, :], mask16[:, t * EXP:(t + 1) * EXP],
                                start=(t == 0), stop=(t == NT - 1))
            ins.then_inc(rank_ps, 1)
            pe.wait_ge(gates_ready, 1)
            for t in range(NT):
                if t >= 2:
                    pe.wait_ge(gt_saved, t - 1)
                pe.transpose(bank[t % 2][0:EXP, 0:P], gates[:, t, :], ident[:, :]).then_inc(gt_ps, 1)
            pe.wait_ge(route_ready, 1)
            pe.wait_ge(b2_in, 16)
            for t in range(NT):
                r = rows(t)
                pe.wait_ge(gt_saved, t + 1)
                if t >= 2:
                    pe.wait_ge(gb_added, t - 1)
                pe.matmul(bank[2 + t % 2][0:r, :], gates_t[:, t * P:t * P + r], b2_sb[:, :],
                          start=True, stop=True).then_inc(gb_ps, 1)
            pe.wait_ge(gb_added, NT)

            def turn_rows(a):
                for k in range(KD):
                    ins = pe.transpose(bank[4 + a][:, k * P:(k + 1) * P], xg[:, a, k * P:(k + 1) * P], ident[:, :])
                ins.then_inc(xgt_ps[a], 1)

            for a in range(2):
                pe.wait_ge(xg_in[a], 16)
                turn_rows(a)
            n = pe.value_load(npair[0:1, 0:1], min_val=1, max_val=(MAXT - 1) // 2)
            with pe.Fori(0, n) as j:
                e = [pe.value_load(te[0:1, bass.ds(2 * j + a, 1)], min_val=0, max_val=EXP - 1) for a in range(2)]
                for a in range(2):
                    pe.wait_ge(w_ready, e[a] + 1)
                    pe.wait_ge(xgt_saved[a], j + 1)
                    pe.wait_ge(hb_ready[a], j + 1)
                    for k in range(KD):
                        ins = pe.matmul(bank[a][:, 0:DFF], xg_t[:, a, k, :],
                                        arena[:, bass.ds(e[a] * EW + E_BASE + k * DFF, DFF)],
                                        start=(k == 0), stop=(k == KD - 1))
                    ins.then_inc(h_ps[a], 1)
                for a in range(2):
                    pe.wait_ge(hg_ready[a], j + 1)
                    pe.wait_ge(hgt_saved[a], j + 1)
                    for k in range(KF):
                        ins = pe.transpose(bank[2 + a][:, k * P:(k + 1) * P], hg[:, a, k * P:(k + 1) * P], ident[:, :])
                    ins.then_inc(hgt_ps[a], 1)
                    pe.wait_ge(xg_in[a], 16 * (j + 2))
                    pe.wait_ge(xgt_saved[a], j + 1)
                    turn_rows(a)
                for a in range(2):
                    pe.wait_ge(hgt_saved[a], j + 2)
                    pe.wait_ge(y_saved[a], j + 1)
                    for k in range(KF):
                        ins = pe.matmul(bank[6 + a][:, :], hg_t[:, a, k, :],
                                        arena[:, bass.ds(e[a] * EW + E_BASE + KD * DFF + k * D, D)],
                                        start=(k == 0), stop=(k == KF - 1))
                    ins.then_inc(y_ps[a], 1)


def kernel(x, src, dst, L0_gnn_W1, L0_gnn_b1, L0_gnn_W2, L0_gnn_b2, L0_gnn_eps, L0_mix_W_qkv, L0_mix_W_out,
           L0_mix_b_out, L0_ffn_router_w, L0_ffn_router_b, L0_ffn_w1, L0_ffn_b1, L0_ffn_w2, L0_ffn_b2):
    import numpy as np
    import concourse.bacc as bacc
    from concourse.bass_utils import run_bass_kernel_spmd

    def by_partition(w):
        w = np.asarray(w)
        return np.ascontiguousarray(w.reshape(-1, P, w.shape[1]).transpose(1, 0, 2))

    w1t = np.asarray(L0_ffn_w1).transpose(0, 2, 1).reshape(EXP, KD, P, DFF).transpose(0, 2, 1, 3).reshape(EXP, P, -1)
    w2t = np.asarray(L0_ffn_w2).transpose(0, 2, 1).reshape(EXP, KF, P, D).transpose(0, 2, 1, 3).reshape(EXP, P, -1)
    arrays = {
        "x": x, "src": src, "dst": dst,
        "wqkv": by_partition(np.asarray(L0_mix_W_qkv).T), "wo": by_partition(np.asarray(L0_mix_W_out).T),
        "bo": L0_mix_b_out, "gw1": by_partition(L0_gnn_W1), "gb1": np.asarray(L0_gnn_b1).reshape(KH, P).T,
        "gw2": by_partition(L0_gnn_W2), "gb2": L0_gnn_b2, "geps": L0_gnn_eps,
        "rw": by_partition(np.asarray(L0_ffn_router_w).T), "rb": L0_ffn_router_b,
        "ew": np.concatenate([w1t, w2t], axis=2), "eb1": np.asarray(L0_ffn_b1).reshape(-1), "eb2": L0_ffn_b2,
    }
    arrays = {f"in_{k}": np.ascontiguousarray(a) for k, a in arrays.items()}
    nc = bacc.Bacc("TRN2", target_bir_lowering=False, num_devices=1)
    args = [nc.dram_tensor(k, a.shape, mybir.dt.from_np(a.dtype), kind="ExternalInput").ap() for k, a in arrays.items()]
    out = nc.dram_tensor("out", (N, D), mybir.dt.float32, kind="ExternalOutput").ap()
    layer(nc, *args, out)
    r = run_bass_kernel_spmd(nc, [arrays], core_ids=[0])
    return r.results[0]["out"]
```

```python
from contextlib import ExitStack

import concourse.bass as bass
from concourse import mybir

P = 128
N = 1250
D = 512
NT = 10
LAST = N - (NT - 1) * P
KD = D // P
HEADS, DH = 8, 64
PAIRS = HEADS // 2
BLOCKS = [(0, 418), (418, 416), (834, 416)]
BW = 418
FC_TILES = [range(0, 3), range(3, 6), range(6, 8), range(8, 10)]
HID = 1024
KH = HID // P
EDGES = 40000
CE = 125
CP = 80
CJ = 4
NC = CP * CJ
WD = 32
NW = NT * P // WD
WPG = P // WD
WCOL = NT * WD
RING = 6
WBUF = 4
OHW = P + WCOL
USUAL = [-(-EDGES * min(WD, N - w * WD) // (N * CE)) + 1 for w in range(NW)]
FIRST = [sum(USUAL[:w]) for w in range(NW + 1)]
EXP = 16
DFF = 256
KF = DFF // P
EW = KD * DFF + KF * D
MAXT = 2 * N // P + EXP + 5
EPS = 1e-5
SCALE = DH ** -0.5
FAR = 1000.0


def layer(nc, x, src, dst, wqkv, wo, bo, gw1, gb1, gw2, gb2, geps, rw, rb, ew, eb1, eb2, out):
    f32r = mybir.dt.float32r
    f32, f16, bf16, i32 = mybir.dt.float32, mybir.dt.float16, mybir.dt.bfloat16, mybir.dt.int32
    ALU = mybir.AluOpType
    ACT = mybir.ActivationFunctionType
    X = mybir.AxisListType.X

    xs = nc.dram_tensor("slots", [MAXT * P, D], f32, kind="Internal").ap()

    with ExitStack() as ctx:
        def sb(name, shape, dt=f32):
            return ctx.enter_context(nc.sbuf_tensor(name, shape, dt))

        def sem(name):
            return ctx.enter_context(nc.semaphore(name))

        SLAB = 198848
        SLAB_AT = -(-nc.sbuf_base // 32) * 32
        arena = sb("arena", [P, SLAB // 4])

        def at(a, shape, parts=P):
            n = 1
            for s in shape:
                n *= s
            v = arena[0:parts, a // 4:a // 4 + n]
            if len(shape) == 2:
                v = v.rearrange("p (a b) -> p a b", b=shape[1])
            if len(shape) == 3:
                v = v.rearrange("p (a b c) -> p a b c", b=shape[1], c=shape[2])
            return v

        def split_tensor(name, a, shape):
            return nc.alloc_sbuf_tensor_at(name, [P] + shape, f32r, offset=SLAB_AT + a, align_bytes=8)

        A_T, RINGB, VALB = 0, 10240, 24576
        XN, RSTT, SET0 = 27216, 47696, 68176
        SETB = 3 * 4 * N + 120
        TMPK = SET0 + SETB
        SET1 = 88416
        PROBS = SET1 + SETB
        NPB = 4
        RSTB = RINGB + 6400
        SPAREB = RSTB + 4 * D
        QT, KT, VT = 117408, 137408, 157888
        xn = at(XN, [NT, D])
        zeros = at(VT, [D])
        a_t = at(A_T, [2, NT, P])
        marks = at(A_T + 2400, [2, NW, CJ], parts=CP)
        marks2 = at(A_T + 3700, [2 * NW], parts=CP)
        val_f = at(A_T + 4400, [500], parts=CP)
        ring = at(RINGB, [RING * OHW // 2], parts=CE).bitcast(f16)
        src_i, dst_i, hi_i, lo_i, win_i, off_i = (
            at(RINGB + 2000 * a, [500], parts=CP).bitcast(i32) for a in range(6))
        lo_f = at(RINGB + 12000, [500], parts=CP)
        NCP = NC + max(USUAL)
        window_cols = at(RINGB + RING * OHW * 2, [WBUF, 2, max(USUAL)], parts=CE)
        val = at(VALB, [NCP], parts=CE)
        low = at(VALB + 4 * NCP, [NCP], parts=CE)
        edge_cols = at(VALB, [2, NCP], parts=CE)
        xn_t = at(RSTT, [KD, NT * P])
        rst_t = at(RSTT, [KD, NT * P])
        k_hl = [split_tensor(f"k_hl{i}", b, [N]) for i, b in enumerate((SET0, SET1))]
        q_hi = [split_tensor(f"q_hi{i}", b + 4 * N, [N]) for i, b in enumerate((SET0, SET1))]
        q_lo = [split_tensor(f"q_lo{i}", b + 8 * N, [N]) for i, b in enumerate((SET0, SET1))]
        k_lo = split_tensor("k_lo", TMPK, [N])
        p_hi = split_tensor("p_hi", PROBS, [NPB, BW])
        p_lo = split_tensor("p_lo", PROBS + NPB * 4 * BW, [NPB, BW])
        rst = at(RSTB, [D])
        spare = at(SPAREB, [OHW // 2], parts=CE).bitcast(f16)
        q_t = at(QT, [PAIRS, N])
        k_t = at(KT, [PAIRS, NT * P])
        v_hl = split_tensor("v_hl", VT, [NT, HEADS, 2, DH])
        w_qkv = at(SET1, [KD, 3 * D])
        WO, W2RAW, W1RAW, HHI = SET0, SET0 + 8192, SET0 + 24576, SET0 + 40960
        w_o = at(WO, [KD, D])
        w1, w2 = at(W1RAW, [KD, HID]), at(W2RAW, [KH, D])
        w2_lo = split_tensor("w2_lo", W2RAW, [KH, D])

        def w2_hi(m):
            return v_hl[:, m // 2, 4 * (m % 2):4 * (m % 2) + 4, :, :].rearrange("p a b c -> p (a b c)")

        HB = 3 * P
        h_hi = split_tensor("h_hi", HHI, [KH, HB])
        h_lo = split_tensor("h_lo", HHI + 4 * KH * HB, [KH, HB])
        h_32 = at(HHI + 4 * KH * HB, [KH, HB])
        xr = at(VT + NT * D * 4, [NT, D])
        x2n_t = at(VT + NT * D * 4 - 4096, [2, KD, P])
        x2n = at(XN, [NT, D])
        E_BASE = 16384 // 4
        b1_all = at(0, [EXP * DFF])
        S = 4 * (E_BASE + EXP * EW)
        xg = at(S, [2, D])
        xg_t = at(S + 4096, [2, KD, P])
        hb = at(S + 8192, [2, DFF])
        hg = at(S + 10240, [2, DFF])
        hg_t = at(S + 12288, [2, KF, P])
        y_sb = at(S + 14336, [2, D])
        gates_t = at(S + 18432, [NT * P], parts=EXP)
        yg = at(0, [2, NT, D])
        R0 = S + 18432 + 4 * NT * P

        def small(k, *shape):
            return at(R0 + 640 * k, list(shape))

        logits, prob, tmp, oh1, oh2, rank, gates = (small(k, NT, EXP) for k in range(7))
        tcmp = at(R0, [MAXT, EXP])
        cum = at(R0, [EXP, EXP])
        total = at(R0 + 4480, [EXP])
        ntile = at(R0 + 4544, [EXP])
        tstart = at(R0 + 4608, [EXP])
        tend = at(R0 + 4672, [EXP])
        red, red2, red3, sums_red = (at(R0 + 4736 + 40 * k, [NT]) for k in range(4))
        tef = at(R0 + 4896, [MAXT])
        many = at(R0 + 5072, [EXP, NT])

        ident = sb("ident", [P, P])
        spare_col = sb("spare_col", [CE, 2, 1])
        bias_b2, bias_bo = sb("bias_b2", [P, D]), sb("bias_bo", [P, D])
        iota16 = sb("iota16", [P, WCOL], f16)
        tri = sb("tri", [P, P], bf16)
        ones = sb("ones", [P, P], bf16)
        mask16 = sb("mask16", [P, NT * EXP], bf16)
        win_idx = sb("win_idx", [CP, NW])
        chunk_idx = sb("chunk_idx", [CP, CJ])
        chunk_neg = sb("chunk_neg", [CP, CJ])
        first5 = sb("first5", [CP, CJ])
        last5 = sb("last5", [CP, CJ])
        mincol = sb("mincol", [CP, 1])
        minrow = sb("minrow", [1, 2 * NW])
        bounds = sb("bounds", [1, NW, 2], i32)
        extras = sb("extras", [1, NW // 2], i32)
        valid = sb("valid", [P, NT])
        einv = sb("einv", [P, EXP])
        thr = sb("thr", [P, NT])
        tidx = sb("tidx", [P, MAXT])
        below = sb("below", [P, EXP, EXP])
        eps_c = sb("eps_c", [P, 1])
        eps1 = sb("eps1", [P, 1])
        b1 = sb("b1", [P, KH])
        rw_sb = sb("rw_sb", [P, KD, EXP])
        rb_sb = sb("rb_sb", [P, EXP])
        b2_sb = sb("b2_sb", [EXP, D])
        stats = sb("stats", [P, NT, 6])
        mv = sb("mv", [P, NT, 2])
        std = sb("std", [P, NT])
        rstd = sb("rstd", [P, NT])
        gate = sb("gate", [P, 2, NT])
        slot = sb("slot", [P, 2, NT], i32)
        te = sb("te", [P, MAXT], i32)
        npair = sb("npair", [P, 1], i32)

        bank = [ctx.enter_context(nc.psum_tensor(f"bank{i}", [P, 512], f32)) for i in range(8)]
        NQB, AV, AW, NB = 3, 3, (5, 7), 6

        x_in = [sem(f"x_in{i}") for i in range(3)]
        edges_in, bias_in, b1_in, rw_in, rb_in, b2_in, eps_in = (
            sem(s) for s in ("edges_in", "bias_in", "b1_in", "rw_in", "rb_in", "b2_in", "eps_in"))
        x_again = sem("x_again")
        wqkv_in, w1_in, w2_in, wo_in, eb1_in = (sem(s) for s in ("wqkv_in", "w1_in", "w2_in", "wo_in", "eb1_in"))
        ew_in = [sem(f"ew_in{e}") for e in range(EXP)]
        zero_filled = sem("zero_filled")
        xpad_ready, zeros_ready, pool_chain, consts_ready = (
            sem(s) for s in ("xpad_ready", "zeros_ready", "pool_chain", "consts_ready"))
        base_ready = sem("base_ready")
        dve_chain, var_ready, std_ready, xn_ready = (sem(s) for s in ("dve_chain", "var_ready", "std_ready", "xn_ready"))
        xnt_ps, xnt_saved = sem("xnt_ps"), sem("xnt_saved")
        proj_ps, proj_saved = sem("proj_ps"), sem("proj_saved")
        edge_ready, edge_ps, edge_saved, min_ps = (sem(s) for s in ("edge_ready", "edge_ps", "edge_saved", "min_ps"))
        marks_ready, mins_ps, mincol_ready, bounds_ready = (
            sem(s) for s in ("marks_ready", "mins_ps", "mincol_ready", "bounds_ready"))
        onehots_ready, onehots_used = sem("onehots_ready"), sem("onehots_used")
        spare_ready, spare_used = sem("spare_ready"), sem("spare_used")
        spare_chain, spare_waited = sem("spare_chain"), sem("spare_waited")
        chunks_ready, cols_ready = sem("chunks_ready"), sem("cols_ready")
        window_saved = sem("window_saved")
        neigh_ps, rst_ready, rstt_ps, rstt_saved = (sem(s) for s in ("neigh_ps", "rst_ready", "rstt_ps", "rstt_saved"))
        qk_ps, p_hi_ready, p_lo_ready, av_step, av_half, av_saved = (
            sem(s) for s in ("qk_ps", "p_hi_ready", "p_lo_ready", "av_step", "av_half", "av_saved"))
        v_hi_ready, v_lo_ready = sem("v_hi_ready"), sem("v_lo_ready")
        head_split = sem("head_split")
        head_ready = [sem(f"head_ready{h}") for h in range(HEADS)]
        out_ps, out_added = sem("out_ps"), sem("out_added")
        w2_hi_ready, w2_lo_ready = sem("w2_hi_ready"), sem("w2_lo_ready")
        hid_ps, hid_hi, hid_lo = sem("hid_ps"), sem("hid_hi"), sem("hid_lo")
        mix_ps, x2_ready = sem("mix_ps"), sem("x2_ready")
        var2_ready, std2_ready, x2n_ready, x2nt_ps, x2nt_saved, logit_ps = (
            sem(s) for s in ("var2_ready", "std2_ready", "x2n_ready", "x2nt_ps", "x2nt_saved", "logit_ps"))
        shifted_ready, exp_ready, mask_ready, rank_ps, route_ready = (
            sem(s) for s in ("shifted_ready", "exp_ready", "mask_ready", "rank_ps", "route_ready"))
        gates_ready, gt_ps, gt_saved, gb_ps, gb_added = (
            sem(s) for s in ("gates_ready", "gt_ps", "gt_saved", "gb_ps", "gb_added"))
        scattered, w_ready = sem("scattered"), sem("w_ready")
        xg_in = [sem(f"xg_in{i}") for i in range(2)]
        xgt_ps = [sem(f"xgt_ps{i}") for i in range(2)]
        xgt_saved = [sem(f"xgt_saved{i}") for i in range(2)]
        h_ps = [sem(f"h_ps{i}") for i in range(2)]
        hb_ready = [sem(f"hb_ready{i}") for i in range(2)]
        hg_ready = [sem(f"hg_ready{i}") for i in range(2)]
        hgt_ps = [sem(f"hgt_ps{i}") for i in range(2)]
        hgt_saved = [sem(f"hgt_saved{i}") for i in range(2)]
        y_ps = [sem(f"y_ps{i}") for i in range(2)]
        y_saved = [sem(f"y_saved{i}") for i in range(2)]
        y_stored = [sem(f"y_stored{i}") for i in range(2)]
        yg_in = [sem(f"yg_in{t}") for t in range(NT)]
        rows_stored, res_ready, stored = sem("rows_stored"), sem("res_ready"), sem("stored")

        def rows(t):
            return LAST if t == NT - 1 else P

        projections = [(which, p, b) for p in range(PAIRS) for which in ("k", "q") for b in range(len(BLOCKS))]
        NPROJ = len(projections)
        steps = [(h, b, t) for h in range(HEADS) for b in range(len(BLOCKS)) for t in range(NT)]
        NS = len(steps)
        SPH = len(BLOCKS) * NT
        NPRE = NPROJ + NT
        PREP, FROM, EARLY = 3, 8, 8
        EVERY = 6.7
        pe_after, act_after, dve_after = ([[] for _ in range(NPRE + NS)] for _ in range(3))

        def start(w):
            return FROM + w * (NPRE - FROM) / EARLY if w < EARLY else NPRE + (w - EARLY) * EVERY

        for w in range(NW):
            for k in range(USUAL[w]):
                made = int(start(w) + k * (start(w + 1) - start(w)) / USUAL[w])
                dve_after[made].append(("pair", w, k))
                if w % 2 == 0 and k == USUAL[w] - 1:
                    held = ("pair", w, k)
                elif w % 2 == 1 and k == 0:
                    pe_after[made + 1] += [("pair", w, k), ("spare", w - 1), held]
                    act_after[made + (2 if made + 2 < NPRE else 4)].append(("window", w - 1))
                else:
                    pe_after[made + 1].append(("pair", w, k))
            if w % 2 == 1:
                act_after[made + (2 if made + 2 < NPRE else 4)].append(("window", w))
            if w % WPG == WPG - 1:
                g = w // WPG
                for t in range(NT):
                    pe_after[made + 5 + t].append(("sum", g, t))
                dve_after[made + NT + 6].append(("sum", g))
                pe_after[made + NT + 7].append(("turn", g))
                act_after[made + NT + 10].append(("turn", g))

        block = ctx.enter_context(nc.Block())

        @block.sync
        def _(sp):
            xv = x[0:(NT - 1) * P, :].rearrange("(t p) d -> p t d", p=P)
            sp.dma_start(xr[:, 0:5, :], xv[:, 0:5, :]).then_inc(x_in[0], 16)
            sp.dma_start(xr[:, 5:9, :], xv[:, 5:9, :]).then_inc(x_in[1], 16)
            sp.wait_ge(xpad_ready, 1)
            sp.dma_start(xr[0:LAST, NT - 1, :], x[(NT - 1) * P:N, :]).then_inc(x_in[2], 16)
            for k in range(KD):
                sp.dma_start(w_qkv[:, k, :], wqkv[:, k, :]).then_inc(wqkv_in, 16)
            sp.wait_ge(zeros_ready, 1)
            sp.dma_start(xs.rearrange("(t p) d -> p t d", p=P),
                         zeros.unsqueeze(1).to_broadcast([P, MAXT, D])).then_inc(zero_filled, 16)
            for h in range(HEADS):
                own, other = slice(DH * (h % 2), DH * (h % 2) + DH), slice(DH - DH * (h % 2), 2 * DH - DH * (h % 2))
                sp.wait_ge(head_split, h + 1)
                for to, of in ((k_hl[h % 2], k_lo), (q_hi[h % 2], q_hi[h % 2]), (q_lo[h % 2], q_lo[h % 2])):
                    sp.dma_start(to[other, :].bitcast(f32), of[own, :].bitcast(f32)).then_inc(head_ready[h], 16)
            sp.wait_ge(qk_ps, SPH * (HEADS - 1))
            sp.dma_start(w_o[:, :, :], wo).then_inc(wo_in, 16)

            def expert(e):
                sp.dma_start(arena[:, E_BASE + e * EW:E_BASE + (e + 1) * EW], ew[e]).then_inc(ew_in[e], 16)

            sp.wait_ge(av_step, NS)
            sp.dma_start(xr[:, 0:9, :], xv).then_inc(x_again, 16)
            sp.wait_ge(xpad_ready, 2)
            sp.dma_start(xr[0:LAST, NT - 1, :], x[(NT - 1) * P:N, :]).then_inc(x_again, 16)
            sp.dma_start(w1[:, :, :], gw1).then_inc(w1_in, 16)
            sp.dma_start(w2[:, :, :], gw2).then_inc(w2_in, 16)
            sp.wait_ge(rstt_ps, NT)
            for e in (0, EXP - 1):
                expert(e)
            sp.wait_ge(hid_ps, KH * len(FC_TILES))
            for e in (4, 5, 6):
                expert(e)
            sp.wait_ge(mix_ps, NT)
            sp.dma_start(b1_all, eb1.partition_broadcast(P)).then_inc(eb1_in, 16)
            for e in range(7, EXP - 1):
                expert(e)
            sp.wait_ge(scattered, 16 * 2 * NT)
            sp.wait_ge(zero_filled, 16)
            for a in range(2):
                sp.dma_start(xg[:, a, :], xs[a * P:(a + 1) * P, :]).then_inc(xg_in[a], 16)
            for e in (1, 2, 3):
                expert(e)
            for a in range(2):
                sp.wait_ge(xgt_ps[a], 1)
                sp.dma_start(xg[:, a, :], xs[(2 + a) * P:(3 + a) * P, :]).then_inc(xg_in[a], 16)
            n = sp.value_load(npair[0:1, 0:1], min_val=1, max_val=(MAXT - 3) // 2)
            with sp.Fori(0, n) as j:
                for a in range(2):
                    sp.wait_ge(xgt_ps[a], j + 2)
                    sp.dma_start(xg[:, a, :], xs[bass.ds((2 * j + 4 + a) * P, P), :]).then_inc(xg_in[a], 16)
                for a in range(2):
                    sp.wait_ge(y_saved[a], j + 2)
                    sp.dma_start(xs[bass.ds((2 * j + a) * P, P), :], y_sb[:, a, :]).then_inc(y_stored[a], 16)
            for a in range(2):
                sp.wait_ge(xg_in[a], 16 * (n + 2))
            for t in range(NT):
                sp.wait_ge(res_ready, t + 1)
                sp.dma_start(out[t * P:t * P + rows(t), :], xr[0:rows(t), t, :]).then_inc(stored, 16)
            sp.wait_ge(stored, 16 * NT)

        @block.gpsimd
        def _(pool):
            count = [0]

            def link(ins):
                count[0] += 1
                ins.then_inc(pool_chain, 1)
                pool.wait_ge(pool_chain, count[0])

            link(pool.memset(xr[96:P, NT - 1, :], 0.0))
            pool.sem_inc(xpad_ready, 1)
            pool.dma_start(dst_i, dst.rearrange("(p n) -> p n", p=CP)).then_inc(edges_in, 16)
            pool.dma_start(src_i, src.rearrange("(p n) -> p n", p=CP)).then_inc(edges_in, 16)
            pool.dma_start(bias_b2[:, :], gb2.partition_broadcast(P)).then_inc(bias_in, 16)
            pool.dma_start(bias_bo[:, :], bo.partition_broadcast(P)).then_inc(bias_in, 16)
            pool.dma_start(b1[:, :], gb1).then_inc(b1_in, 16)
            pool.dma_start(rw_sb[:, :, :], rw).then_inc(rw_in, 16)
            pool.dma_start(rb_sb[:, :], rb.partition_broadcast(P)).then_inc(rb_in, 16)
            pool.dma_start(eps_c[:, :], geps.partition_broadcast(P)).then_inc(eps_in, 16)
            pool.dma_start(b2_sb[:, :], eb2).then_inc(b2_in, 16)
            link(pool.memset(ident[:, :], 0.0))
            link(pool.affine_select(out=ident[:, :], in_=ident[:, :], compare_op=ALU.not_equal, fill=1.0,
                                    base=0, pattern=[[-1, P]], channel_multiplier=1))
            pool.sem_inc(consts_ready, 1)
            link(pool.memset(zeros, 0.0))
            pool.sem_inc(zeros_ready, 1)
            link(pool.memset(tri[:, :], 1.0))
            link(pool.affine_select(out=tri[:, :], in_=tri[:, :], compare_op=ALU.is_ge, fill=0.0,
                                    base=-1, pattern=[[1, P]], channel_multiplier=-1))
            link(pool.memset(valid[:, :], 1.0))
            link(pool.affine_select(out=valid[:, NT - 1:NT], in_=valid[:, NT - 1:NT], compare_op=ALU.is_ge,
                                    fill=0.0, base=LAST - 1, pattern=[[0, 1]], channel_multiplier=-1))
            link(pool.memset(below[:, :, :], 1.0))
            link(pool.affine_select(out=below[:, :, :], in_=below[:, :, :], compare_op=ALU.is_ge, fill=0.0,
                                    base=-1, pattern=[[1, EXP], [-1, EXP]], channel_multiplier=0))
            link(pool.memset(ones[:, :], 1.0))

            def ramp(t, pattern, base=0, per_partition=0):
                link(pool.iota(t, pattern=pattern, base=base, channel_multiplier=per_partition,
                               allow_small_or_imprecise_dtypes=True))

            ramp(iota16[:, :], [[1, WCOL]])
            ramp(win_idx[:, :], [[1, NW]])
            ramp(chunk_idx[:, :], [[1, CJ]], 0, CJ)
            ramp(chunk_neg[:, :], [[-1, CJ]], 0, -CJ)
            ramp(einv[:, :], [[-1, EXP]], EXP)
            ramp(thr[:, :], [[P, NT]])
            ramp(tidx[:, :], [[1, MAXT]])
            pool.sem_inc(consts_ready, 1)
            pool.wait_ge(bias_in, 32)
            link(pool.tensor_tensor(bias_b2[:, :], bias_b2[:, :], bias_bo[:, :], ALU.add))
            def split_head(h):
                p, own, i = h // 2, slice(DH * (h % 2), DH * (h % 2) + DH), h % 2
                pool.wait_ge(proj_saved, 6 * (p + 1))
                if h >= 1:
                    pool.wait_ge(head_ready[h - 1], 48)
                if h >= 2:
                    pool.wait_ge(qk_ps, SPH * (h - 1))
                if h == 1:
                    pool.wait_ge(proj_ps, NPROJ + NT)
                link(pool.tensor_copy(k_hl[i][own, :], k_t[own, p, 0:N]))
                link(pool.tensor_tensor(k_lo[own, :], k_t[own, p, 0:N], k_hl[i][own, :].bitcast(f32), ALU.subtract))
                link(pool.tensor_copy(q_hi[i][own, :], q_t[own, p, :]))
                link(pool.tensor_tensor(q_lo[i][own, :], q_t[own, p, :], q_hi[i][own, :].bitcast(f32), ALU.subtract))
                pool.sem_inc(head_split, 1)

            def window_columns(w):
                if w == 0:
                    pool.wait_ge(chunks_ready, 1)
                if w >= WBUF:
                    pool.wait_ge(onehots_ready, FIRST[w - WBUF + 1])
                n = USUAL[w]
                lo = pool.value_load(bounds[0:1, w, 0:1], min_val=0, max_val=NC - 1)
                to = window_cols[:, w % WBUF, :, 0:n]
                link(pool.tensor_copy(to, edge_cols[:, :, bass.ds(lo, n)]))
                link(pool.tensor_scalar(to[:, 0, :], to[:, 0, :], float(-WCOL * w), None, ALU.add))
                pool.sem_inc(cols_ready, 1)

            pairs, links, chunk = (pool.alloc_register(f"pool_{s}") for s in ("pairs", "links", "chunk"))
            pool.reg_mov(pairs, 0)
            pool.reg_mov(links, 0)

            def link_spare(ins):
                ins.then_inc(spare_chain, 1)
                pool.reg_add(links, links, 1)
                pool.wait_ge(spare_chain, pool.snap(links, min_val=1, max_val=2 * NW * NC))
                pool.sem_inc(spare_waited, 1)

            def spare_chunks(w):
                both = pool.value_load(extras[0:1, w // 2:w // 2 + 1], min_val=0, max_val=2 * NC)
                with pool.If(both > 0):
                    for v in (w, w + 1):
                        spare_window(v)

            def spare_window(w):
                extra = pool.value_load(bounds[0:1, w, 1:2], min_val=0, max_val=NC)
                with pool.If(extra > 0):
                    lo = pool.value_load(bounds[0:1, w, 0:1], min_val=0, max_val=NC - 1)
                    pool.reg_mov(chunk, lo + USUAL[w])
                    with pool.Fori(0, extra):
                        pool.wait_ge(spare_used, pool.snap(pairs, min_val=0, max_val=NW * NC) + 1)
                        pool.sem_inc(spare_waited, 1)
                        link_spare(pool.tensor_copy(
                            spare_col[:, :, :], edge_cols[:, :, bass.ds(pool.snap(chunk, min_val=0, max_val=NC - 1), 1)]))
                        link_spare(pool.tensor_scalar(spare_col[:, 0, :], spare_col[:, 0, :], float(-WCOL * w), None,
                                                      ALU.add))
                        pool.tensor_scalar(spare[:, 0:P], iota16[0:CE, 0:P], spare_col[:, 1, :], None, ALU.is_equal)
                        pool.tensor_scalar(spare[:, P:OHW], iota16[0:CE, :], spare_col[:, 0, :], None,
                                           ALU.is_equal).then_inc(spare_ready, 1)
                        pool.reg_add(pairs, pairs, 1)
                        pool.reg_add(chunk, chunk, 1)
                    pool.wait_ge(spare_ready, pool.snap(pairs, min_val=1, max_val=NW * NC))
                    pool.sem_inc(spare_waited, 1)

            for _, what, i in sorted([(start(0) + 0.5 if h == 0 else NPRE + SPH * (h - 1) + 1, "head", h) for h in range(HEADS)]
                                     + [(start(max(w - 2, 0)), "cols", w) for w in range(NW)]
                                     + [(start(w), "spare", w) for w in range(0, NW, 2)]):
                {"head": split_head, "cols": window_columns, "spare": spare_chunks}[what](i)
            pool.wait_ge(av_step, NS)
            link(pool.memset(xr[96:P, NT - 1, :], 0.0))
            pool.sem_inc(xpad_ready, 1)
            pool.wait_ge(x_again, 32)
            for t in range(NT):
                link(pool.tensor_tensor(xr[:, t, :], xr[:, t, :], xn[:, t, :], ALU.add))
                pool.sem_inc(base_ready, 1)
            pool.wait_ge(route_ready, 1)
            pool.wait_ge(zero_filled, 16)
            for t in range(NT):
                for k in range(2):
                    pool.indirect_dma_start(
                        out=xs, out_offset=bass.IndirectOffsetOnAxis(ap=slot[0:rows(t), k, t:t + 1], axis=0),
                        in_=x2n[0:rows(t), t, :], in_offset=None).then_inc(scattered, 16)
            for e in range(EXP):
                pool.wait_ge(ew_in[e], 16)
                pool.sem_inc(w_ready, 1)
            n = pool.value_load(npair[0:1, 0:1], min_val=1, max_val=(MAXT - 3) // 2)
            for a in range(2):
                pool.wait_ge(y_stored[a], 16 * n + 16)
                pool.sem_inc(rows_stored, 1)
            pool.wait_ge(rows_stored, 2)
            for t in range(NT):
                for k in range(2):
                    pool.indirect_dma_start(
                        out=yg[0:rows(t), k, t, :], out_offset=None, in_=xs,
                        in_offset=bass.IndirectOffsetOnAxis(ap=slot[0:rows(t), k, t:t + 1], axis=0)
                    ).then_inc(yg_in[t], 16)

        @block.scalar
        def _(act):
            copy = ACT.Copy
            for half in range(2):
                act.wait_ge(var_ready, half + 1)
                act.activation(std[:, 5 * half:5 * half + 5], std[:, 5 * half:5 * half + 5],
                               ACT.Sqrt).then_inc(std_ready, 1)
            for t in range(NT):
                act.wait_ge(xnt_ps, t + 1)
                act.activation(xn_t[:, :, t * P:(t + 1) * P],
                               bank[6 + t % 2][:, :].rearrange("p (k n) -> p k n", k=KD),
                               copy).then_inc(xnt_saved, 1)
            def graph(turn):
                for what, i in act_after[turn]:
                    if what == "window":
                        act.wait_ge(onehots_used, FIRST[i + 1] + (i + 1) % 2)
                        g = i // WPG
                        if i % WPG == 0 and g >= 2:
                            act.wait_ge(neigh_ps, g - 1)
                        act.activation(a_t[:, g % 2, :, (i % WPG) * WD:(i % WPG + 1) * WD],
                                       bank[AW[i % 2]][:, 0:WCOL].rearrange("p (b d) -> p b d", b=NT),
                                       copy).then_inc(window_saved, 1)
                    else:
                        act.wait_ge(rstt_ps, i + 1)
                        act.activation(rst_t[:, :, i * P:(i + 1) * P],
                                       bank[NB][:, :].rearrange("p (k n) -> p k n", k=KD), copy).then_inc(rstt_saved, 1)

            for g, (which, p, b) in enumerate(projections):
                o, n = BLOCKS[b]
                act.wait_ge(proj_ps, g + 1)
                if which == "k":
                    act.activation(k_t[:, p, o:o + n], bank[g % 5][:, 0:n], copy).then_inc(proj_saved, 1)
                else:
                    act.activation(q_t[:, p, o:o + n], bank[g % 5][:, 0:n], copy, scale=SCALE).then_inc(proj_saved, 1)
                graph(g)
            act.wait_ge(zero_filled, 16)
            for t in range(NT):
                act.wait_ge(proj_ps, NPROJ + t + 1)
                act.activation(v_hl[:, t, :, 0, :], bank[(NPROJ + t) % 5][:, :].rearrange("p (h d) -> p h d", h=HEADS),
                               copy).then_inc(v_hi_ready, 1)
                graph(NPROJ + t)

            def save_attention(m):
                h, b = m // 3, m % 3
                o, n = BLOCKS[b]
                act.wait_ge(av_step, NT * (m + 1))
                act.activation(q_t[DH * (h % 2):DH * (h % 2) + DH, h // 2, o:o + n], bank[AV + m % 2][0:DH, 0:n],
                               copy).then_inc(av_half, 1)

            for s, (h, b, t) in enumerate(steps):
                n = BLOCKS[b][1]
                kt = rows(t)
                act.wait_ge(qk_ps, s + 1)
                if s >= NPB:
                    act.wait_ge(av_step, s - NPB + 1)
                if s == 0:
                    act.wait_ge(proj_ps, NPRE)
                act.activation(p_hi[0:kt, s % NPB, 0:n], bank[s % NQB][0:kt, 0:n], ACT.Relu).then_inc(p_hi_ready, 1)
                if s > NT and s % NT == 1:
                    save_attention(s // NT - 1)
                graph(NPRE + s)
            save_attention(HEADS * 3 - 1)
            act.wait_ge(w2_in, 16)
            act.wait_ge(b1_in, 16)
            g = 0
            for tiles in FC_TILES:
                n = min(N, tiles[-1] * P + P) - tiles[0] * P
                if tiles[0]:
                    act.wait_ge(mix_ps, tiles[0])
                for m in range(KH):
                    if tiles[0] == 0:
                        act.activation(w2_hi(m), w2[:, m, :], copy).then_inc(w2_hi_ready, 1)
                    act.wait_ge(hid_ps, g + 1)
                    act.activation(h_32[:, m, 0:n], bank[g % 4][:, 0:n], ACT.Relu, bias=b1[:, m:m + 1])
                    act.activation(h_hi[:, m, 0:n], bank[g % 4][:, 0:n], ACT.Relu,
                                   bias=b1[:, m:m + 1]).then_inc(hid_hi, 1)
                    g += 1
                for t in tiles:
                    act.wait_ge(var2_ready, t + 1)
                    act.activation(std[:, t:t + 1], std[:, t:t + 1], ACT.Sqrt).then_inc(std2_ready, 1)
                    act.wait_ge(x2nt_ps, t + 1)
                    if t >= 2:
                        act.wait_ge(logit_ps, t - 1)
                    act.activation(x2n_t[:, t % 2, :, :], bank[6][:, :].rearrange("p (k n) -> p k n", k=KD),
                                   copy).then_inc(x2nt_saved, 1)
            act.wait_ge(shifted_ready, 1)
            act.activation(prob[:, :, :], logits[:, :, :], ACT.Exp).then_inc(exp_ready, 1)
            for t in range(NT):
                act.wait_ge(gt_ps, t + 1)
                act.activation(gates_t[:, t * P:(t + 1) * P], bank[t % 2][0:EXP, 0:P], copy).then_inc(gt_saved, 1)
            for a in range(2):
                act.wait_ge(xgt_ps[a], 1)
                act.activation(xg_t[:, a, :, :], bank[4 + a][:, :].rearrange("p (k n) -> p k n", k=KD),
                               copy).then_inc(xgt_saved[a], 1)
            n = act.value_load(npair[0:1, 0:1], min_val=1, max_val=(MAXT - 3) // 2)
            with act.Fori(0, n) as j:
                for a in range(2):
                    act.wait_ge(hb_ready[a], j + 2)
                    act.activation(hg[:, a, :], hb[:, a, :], ACT.Gelu).then_inc(hg_ready[a], 1)
                for a in range(2):
                    act.wait_ge(xgt_ps[a], j + 2)
                    act.activation(xg_t[:, a, :, :], bank[4 + a][:, :].rearrange("p (k n) -> p k n", k=KD),
                                   copy).then_inc(xgt_saved[a], 1)

        @block.vector
        def _(dve):
            count = [0]

            def link(ins):
                count[0] += 1
                ins.then_inc(dve_chain, 1)
                dve.wait_ge(dve_chain, count[0])

            for half in range(2):
                for t in range(5 * half, 5 * half + 5):
                    if t == 0:
                        dve.wait_ge(x_in[0], 16)
                    if t == 5:
                        dve.wait_ge(x_in[1], 16)
                    if t == NT - 1:
                        dve.wait_ge(x_in[2], 16)
                        dve.wait_ge(xpad_ready, 1)
                    ins = dve.bn_stats(stats[:, t, :], xr[:, t, :])
                link(ins)
                for t in range(5 * half, 5 * half + 5):
                    ins = dve.bn_aggr(mv[:, t, :], stats[:, t, :])
                link(ins)
                dve.tensor_scalar_add(std[:, 5 * half:5 * half + 5], mv[:, 5 * half:5 * half + 5, 1],
                                      EPS).then_inc(var_ready, 1)
                dve.wait_ge(std_ready, half + 1)
                link(dve.reciprocal(rstd[:, 5 * half:5 * half + 5], std[:, 5 * half:5 * half + 5]))
                for t in range(5 * half, 5 * half + 5):
                    dve.tensor_scalar(xn[:, t, :], xr[:, t, :], mv[:, t, 0:1], rstd[:, t:t + 1],
                                      ALU.subtract, ALU.mult).then_inc(xn_ready, 1)
            dve.wait_ge(edges_in, 32)
            dve.wait_ge(consts_ready, 2)
            dve.tensor_single_scalar(win_i, dst_i, 5, op=ALU.arith_shift_right)
            dve.tensor_single_scalar(off_i, dst_i, WD - 1, op=ALU.bitwise_and)
            dve.tensor_single_scalar(hi_i, src_i, 7, op=ALU.arith_shift_right)
            link(dve.tensor_single_scalar(lo_i, src_i, P - 1, op=ALU.bitwise_and))
            dve.tensor_copy(lo_f, lo_i).then_inc(edge_ready, 1)
            win_v = win_i.rearrange("p (j n) -> p j n", j=CJ)
            dve.tensor_reduce(first5[:, :], win_v, X, ALU.min)
            dve.tensor_reduce(last5[:, :], win_v, X, ALU.max)
            link(dve.scalar_tensor_tensor(out=val_f, in0=win_i, scalar=float(NT), in1=hi_i,
                                          op0=ALU.mult, op1=ALU.add))
            dve.scalar_tensor_tensor(out=val_f, in0=val_f, scalar=float(WD), in1=off_i,
                                     op0=ALU.mult, op1=ALU.add).then_inc(edge_ready, 1)
            for jj in range(CJ):
                dve.tensor_scalar(marks[:, 0, :, jj], win_idx[:, :], last5[:, jj:jj + 1], FAR, ALU.is_gt, ALU.mult)
                last = dve.tensor_scalar(marks[:, 1, :, jj], win_idx[:, :], first5[:, jj:jj + 1], FAR,
                                         ALU.is_lt, ALU.mult)
            link(last)
            for jj in range(CJ):
                dve.tensor_scalar(marks[:, 0, :, jj], marks[:, 0, :, jj], chunk_idx[:, jj:jj + 1], None, ALU.add)
                last = dve.tensor_scalar(marks[:, 1, :, jj], marks[:, 1, :, jj], chunk_neg[:, jj:jj + 1], None,
                                         ALU.add)
            link(last)
            dve.tensor_reduce(marks2, marks.rearrange("p a w j -> p (a w) j"), X, ALU.min).then_inc(marks_ready, 1)
            dve.wait_ge(mins_ps, 1)
            dve.tensor_reduce(mincol[:, :], bank[AW[0]][0:2 * NW, 0:CP], X, ALU.min).then_inc(mincol_ready, 1)
            dve.wait_ge(min_ps, 1)
            link(dve.tensor_copy(minrow[:, :], bank[NB][0:1, 0:2 * NW]))
            link(dve.tensor_scalar(minrow[:, 0:NW], minrow[:, 0:NW], float(NC - 1), None, ALU.min))
            link(dve.tensor_scalar(minrow[:, NW:2 * NW], minrow[:, NW:2 * NW], -1.0, None, ALU.mult))
            link(dve.tensor_tensor(minrow[:, NW:2 * NW], minrow[:, NW:2 * NW], minrow[:, 0:NW], ALU.max))
            link(dve.tensor_tensor(minrow[:, NW:2 * NW], minrow[:, NW:2 * NW], minrow[:, 0:NW], ALU.subtract))
            for of, usual in ((minrow[:, NW:2 * NW - 1], USUAL[0]), (minrow[:, 2 * NW - 1:2 * NW], USUAL[NW - 1])):
                last = dve.tensor_scalar(of, of, float(1 - usual), 0.0, ALU.add, ALU.max)
            link(last)
            dve.tensor_copy(bounds[:, :, 0], minrow[:, 0:NW])
            dve.tensor_copy(bounds[:, :, 1], minrow[:, NW:2 * NW])
            two = minrow[:, NW:2 * NW].rearrange("p (w a) -> p w a", a=2)
            dve.tensor_tensor(extras[:, :], two[:, :, 0], two[:, :, 1], ALU.add).then_inc(bounds_ready, 1)
            dve.wait_ge(edge_ps, 1)
            dve.tensor_copy(low[:, 0:NC].rearrange("p (c j) -> p j c", j=CJ),
                            bank[AW[0]][0:CE, 0:NC].rearrange("p (j c) -> p j c", j=CJ)).then_inc(edge_saved, 1)
            dve.wait_ge(edge_ps, 2)
            link(dve.tensor_copy(val[:, 0:NC].rearrange("p (c j) -> p j c", j=CJ),
                                 bank[NB][0:CE, 0:NC].rearrange("p (j c) -> p j c", j=CJ)))
            dve.sem_inc(edge_saved, 1)

            dve.wait_ge(eps_in, 16)
            link(dve.tensor_scalar_add(eps1[:, :], eps_c[:, :], 1.0))
            dve.memset(val[:, NC:NCP], -1e6)
            link(dve.memset(low[:, NC:NCP], 0.0))
            dve.wait_ge(bounds_ready, 1)
            dve.sem_inc(chunks_ready, 1)
            def do(what, i, k=0):
                if what == "pair":
                    if k == 0:
                        dve.wait_ge(cols_ready, i + 1)
                    q = FIRST[i] + k
                    if q >= RING:
                        dve.wait_ge(onehots_used, q - RING + 2)
                    at_slot = (q % RING) * OHW
                    dve.tensor_scalar(ring[:, at_slot:at_slot + P], iota16[0:CE, 0:P],
                                      window_cols[:, i % WBUF, 1, k:k + 1], None, ALU.is_equal)
                    dve.tensor_scalar(ring[:, at_slot + P:at_slot + OHW], iota16[0:CE, :],
                                      window_cols[:, i % WBUF, 0, k:k + 1], None,
                                      ALU.is_equal).then_inc(onehots_ready, 1)
                else:
                    dve.wait_ge(neigh_ps, i + 1)
                    if i >= 1:
                        dve.wait_ge(rstt_ps, i)
                    dve.scalar_tensor_tensor(out=rst, in0=xn[:, i, :], scalar=eps1[:, 0:1], in1=bank[NB][:, :],
                                             op0=ALU.mult, op1=ALU.add).then_inc(rst_ready, 1)

            for turn in range(FROM, NPRE):
                if turn >= NPROJ:
                    t = turn - NPROJ
                    dve.wait_ge(v_hi_ready, t + 1)
                    dve.tensor_tensor(v_hl[:, t, :, 1, :],
                                      bank[turn % 5][:, :].rearrange("p (h d) -> p h d", h=HEADS),
                                      v_hl[:, t, :, 0, :].bitcast(f32), ALU.subtract).then_inc(v_lo_ready, 1)
                for what in dve_after[turn]:
                    do(*what)

            def add_attention(m):
                h, b = m // 3, m % 3
                o, n = BLOCKS[b]
                to = q_t[DH * (h % 2):DH * (h % 2) + DH, h // 2, o:o + n]
                dve.wait_ge(av_half, m + 1)
                dve.tensor_tensor(to, to, bank[AV + m % 2][DH:P, 0:n], ALU.add).then_inc(av_saved, 1)

            for s, (h, b, t) in enumerate(steps):
                n = BLOCKS[b][1]
                kt = rows(t)
                dve.wait_ge(p_hi_ready, s + 1)
                dve.scalar_tensor_tensor(out=p_lo[0:kt, s % NPB, 0:n], in0=bank[s % NQB][0:kt, 0:n], scalar=0.0,
                                         in1=p_hi[0:kt, s % NPB, 0:n].bitcast(f32), op0=ALU.max,
                                         op1=ALU.subtract).then_inc(p_lo_ready, 1)
                if s > NT and s % NT == 2:
                    add_attention(s // NT - 1)
                for what in dve_after[NPRE + s]:
                    do(*what)
            add_attention(HEADS * 3 - 1)

            for t in range(NT):
                r = rows(t)
                dve.wait_ge(base_ready, t + 1)
                link(dve.tensor_tensor(xr[:, t, :], xr[:, t, :], bias_b2[:, :], ALU.add))
                dve.wait_ge(out_ps, t + 1)
                dve.tensor_tensor(xr[0:r, t, :], xr[0:r, t, :], bank[(5 + t) % 8][0:r, :], ALU.add).then_inc(out_added, 1)
            dve.wait_ge(out_added, NT)
            g = 0
            for tiles in FC_TILES:
                n = min(N, tiles[-1] * P + P) - tiles[0] * P
                for m in range(KH):
                    if tiles[0] == 0:
                        dve.wait_ge(w2_hi_ready, m + 1)
                        dve.scalar_tensor_tensor(out=w2_lo[:, m, :], in0=w2[:, m, :], scalar=1.0, in1=w2_hi(m).bitcast(f32),
                                                 op0=ALU.mult, op1=ALU.subtract).then_inc(w2_lo_ready, 1)
                    dve.wait_ge(hid_hi, g + 1)
                    dve.tensor_tensor(h_lo[:, m, 0:n], h_32[:, m, 0:n], h_hi[:, m, 0:n].bitcast(f32),
                                      ALU.subtract).then_inc(hid_lo, 1)
                    g += 1
                for t in tiles:
                    r = rows(t)
                    dve.wait_ge(mix_ps, t + 1)
                    link(dve.tensor_tensor(xr[0:r, t, :], xr[0:r, t, :], bank[4 + t % 2][0:r, :], ALU.add))
                    dve.sem_inc(x2_ready, 1)
                    link(dve.bn_stats(stats[:, t, :], xr[:, t, :]))
                    link(dve.bn_aggr(mv[:, t, :], stats[:, t, :]))
                    dve.tensor_scalar_add(std[:, t:t + 1], mv[:, t, 1:2], EPS).then_inc(var2_ready, 1)
                    dve.wait_ge(std2_ready, t + 1)
                    link(dve.reciprocal(rstd[:, t:t + 1], std[:, t:t + 1]))
                    dve.tensor_scalar(x2n[:, t, :], xr[:, t, :], mv[:, t, 0:1], rstd[:, t:t + 1],
                                      ALU.subtract, ALU.mult).then_inc(x2n_ready, 1)

            def over_e(a):
                return a.unsqueeze(2).to_broadcast([P, NT, EXP])

            def over_t(a):
                return a.unsqueeze(1).to_broadcast([P, NT, EXP])

            dve.wait_ge(logit_ps, NT)
            dve.wait_ge(rb_in, 16)
            lg_ps = bank[7][:, 0:NT * EXP].rearrange("p (t e) -> p t e", e=EXP)
            link(dve.tensor_tensor(logits, lg_ps, over_t(rb_sb[:, :]), ALU.add))
            link(dve.tensor_reduce(red, logits, X, ALU.max))
            dve.tensor_tensor(logits, logits, over_e(red), ALU.subtract).then_inc(shifted_ready, 1)
            dve.wait_ge(exp_ready, 1)
            link(dve.tensor_reduce(red2, prob, X, ALU.add))
            link(dve.reciprocal(red3, red2))
            link(dve.tensor_tensor(prob, prob, over_e(red3), ALU.mult))
            for k, oh in ((0, oh1), (1, oh2)):
                link(dve.tensor_reduce(gate[:, k, :], prob, X, ALU.max))
                link(dve.tensor_tensor(tmp, prob, over_e(gate[:, k, :]), ALU.is_equal))
                link(dve.tensor_tensor(tmp, tmp, over_t(einv[:, :]), ALU.mult))
                link(dve.tensor_reduce(red, tmp, X, ALU.max))
                link(dve.tensor_tensor(oh, over_t(einv[:, :]), over_e(red), ALU.is_equal))
                if k == 0:
                    link(dve.scalar_tensor_tensor(out=prob, in0=oh1, scalar=-2.0, in1=prob,
                                                  op0=ALU.mult, op1=ALU.add))
            link(dve.tensor_tensor(tmp, oh1, oh2, ALU.add))
            mask_v = mask16[:, :].rearrange("p (t e) -> p t e", e=EXP)
            link(dve.tensor_tensor(mask_v, tmp, over_e(valid[:, :]), ALU.mult))
            dve.sem_inc(mask_ready, 1)
            dve.tensor_tensor(tmp, oh1, over_e(gate[:, 0, :]), ALU.mult)
            link(dve.tensor_tensor(gates, oh2, over_e(gate[:, 1, :]), ALU.mult))
            link(dve.tensor_tensor(gates, gates, tmp, ALU.add))
            dve.sem_inc(gates_ready, 1)
            dve.wait_ge(rank_ps, 1)
            link(dve.tensor_copy(total, bank[3][:, 0:EXP]))
            link(dve.tensor_tensor(many, total.unsqueeze(2).to_broadcast([P, EXP, NT]),
                                   thr[:, :].unsqueeze(1).to_broadcast([P, EXP, NT]), ALU.is_gt))
            link(dve.tensor_reduce(ntile, many, X, ALU.add))
            link(dve.tensor_tensor(cum, ntile.unsqueeze(1).to_broadcast([P, EXP, EXP]), below[:, :, :], ALU.mult))
            link(dve.tensor_reduce(tstart, cum, X, ALU.add))
            dve.tensor_tensor(tend, tstart, ntile, ALU.add)
            link(dve.tensor_scalar(total, tstart, float(P), None, ALU.mult))
            link(dve.tensor_tensor(rank, bank[2][:, 0:NT * EXP].rearrange("p (t e) -> p t e", e=EXP),
                                   over_t(total), ALU.add))
            for k, oh in ((0, oh1), (1, oh2)):
                link(dve.tensor_tensor(tmp, oh, rank, ALU.mult))
                s_k = (sums_red, red3)[k]
                link(dve.tensor_reduce(s_k, tmp, X, ALU.add))
                last = dve.tensor_copy(slot[:, k, :], s_k)
            link(last)
            link(dve.tensor_scalar(red2[:, 0:1], tend[:, EXP - 1:EXP], 1.0, None, ALU.add))
            link(dve.tensor_copy(npair[:, :], red2[:, 0:1]))
            link(dve.tensor_single_scalar(npair[:, :], npair[:, :], 1, op=ALU.arith_shift_right))
            link(dve.tensor_tensor(tcmp, tidx[:, :].unsqueeze(2).to_broadcast([P, MAXT, EXP]),
                                   tend.unsqueeze(1).to_broadcast([P, MAXT, EXP]), ALU.is_ge))
            link(dve.tensor_reduce(tef, tcmp, X, ALU.add))
            link(dve.tensor_scalar(te[:, :], tef, float(EXP - 1), None, ALU.min))
            dve.sem_inc(route_ready, 1)
            for t in range(NT):
                r = rows(t)
                dve.wait_ge(gb_ps, t + 1)
                dve.tensor_tensor(xr[0:r, t, :], xr[0:r, t, :], bank[2 + t % 2][0:r, :], ALU.add).then_inc(gb_added, 1)
            dve.wait_ge(eb1_in, 16)
            for a in range(2):
                dve.sem_inc(hb_ready[a], 1)
                dve.sem_inc(hgt_saved[a], 1)
                dve.sem_inc(y_saved[a], 1)
                dve.sem_inc(y_stored[a], 16)
            n = dve.value_load(npair[0:1, 0:1], min_val=1, max_val=(MAXT - 3) // 2)
            with dve.Fori(0, n) as j:
                for a in range(2):
                    e = dve.value_load(te[0:1, bass.ds(2 * j + a, 1)], min_val=0, max_val=EXP - 1)
                    dve.wait_ge(h_ps[a], j + 1)
                    dve.tensor_tensor(hb[:, a, :], bank[a][:, 0:DFF], b1_all[:, bass.ds(e * DFF, DFF)],
                                      ALU.add).then_inc(hb_ready[a], 1)
                for a in range(2):
                    dve.wait_ge(hgt_ps[a], j + 1)
                    dve.tensor_copy(hg_t[:, a, :, :],
                                    bank[2 + a][:, 0:KF * P].rearrange("p (k n) -> p k n", k=KF)
                                    ).then_inc(hgt_saved[a], 1)
                for a in range(2):
                    dve.wait_ge(y_ps[a], j + 1)
                    dve.wait_ge(y_stored[a], 16 * j + 16)
                    dve.tensor_copy(y_sb[:, a, :], bank[6 + a][:, :]).then_inc(y_saved[a], 1)
            for t in range(NT):
                r = rows(t)
                dve.wait_ge(yg_in[t], 32)
                link(dve.scalar_tensor_tensor(out=xr[0:r, t, :], in0=yg[0:r, 0, t, :], scalar=gate[0:r, 0, t:t + 1],
                                              in1=xr[0:r, t, :], op0=ALU.mult, op1=ALU.add))
                dve.scalar_tensor_tensor(out=xr[0:r, t, :], in0=yg[0:r, 1, t, :], scalar=gate[0:r, 1, t:t + 1],
                                         in1=xr[0:r, t, :], op0=ALU.mult, op1=ALU.add).then_inc(res_ready, 1)

        @block.tensor
        def _(pe):
            pe.sem_inc(spare_used, 1)
            pe.wait_ge(consts_ready, 2)
            for t in range(NT):
                pe.wait_ge(xn_ready, t + 1)
                if t >= 2:
                    pe.wait_ge(xnt_saved, t - 1)
                for k in range(KD):
                    ins = pe.transpose(bank[6 + t % 2][:, k * P:(k + 1) * P], xn[:, t, k * P:(k + 1) * P], ident[:, :])
                ins.then_inc(xnt_ps, 1)
            pe.wait_ge(xnt_saved, NT)
            pe.wait_ge(wqkv_in, 16 * KD)
            def lay_out_edges(part):
                if part == 0:
                    pe.wait_ge(marks_ready, 1)
                    pe.transpose(bank[AW[0]][0:2 * NW, 0:CP], marks2, ident[0:CP, 0:CP]).then_inc(mins_ps, 1)
                elif part == 1:
                    pe.wait_ge(mincol_ready, 1)
                    pe.transpose(bank[NB][0:1, 0:CP], mincol[:, :], ident[0:CP, 0:CP]).then_inc(min_ps, 1)
                elif part == 2:
                    pe.wait_ge(bounds_ready, 1)
                    pe.wait_ge(edge_ready, 2)
                    for bk, of in ((AW[0], lo_f), (NB, val_f)):
                        for jj in range(CJ):
                            ins = pe.transpose(bank[bk][0:CE, jj * CP:(jj + 1) * CP], of[:, jj * CE:(jj + 1) * CE],
                                               ident[0:CP, 0:CP])
                        ins.then_inc(edge_ps, 1)

            pairs = pe.alloc_register("pe_pairs")
            pe.reg_mov(pairs, 0)

            def product(w, of, at_slot, start, stop):
                return pe.matmul(bank[AW[w % 2]][:, 0:WCOL], of[:, at_slot:at_slot + P],
                                 of[:, at_slot + P:at_slot + OHW], start=start, stop=stop, skip_group_check=True)

            def count_pair(w, k):
                if k == 0 and w >= 2:
                    pe.wait_ge(window_saved, w - 1)
                q = FIRST[w] + k
                pe.wait_ge(onehots_ready, q + 1)
                product(w, ring, (q % RING) * OHW, k == 0, k == USUAL[w] - 1).then_inc(onehots_used, 1)

            def count_spare(w):
                both = pe.value_load(extras[0:1, w // 2:w // 2 + 1], min_val=0, max_val=2 * NC)
                with pe.If(both > 0):
                    for v in (w, w + 1):
                        extra = pe.value_load(bounds[0:1, v, 1:2], min_val=0, max_val=NC)
                        with pe.If(extra > 0):
                            with pe.Fori(0, extra):
                                pe.wait_ge(spare_ready, pe.snap(pairs, min_val=0, max_val=NW * NC) + 1)
                                product(v, spare, 0, False, False).then_inc(spare_used, 1)
                                pe.reg_add(pairs, pairs, 1)

            def neighbours(g, t):
                if t == 0:
                    pe.wait_ge(window_saved, WPG * (g + 1))
                    if g:
                        pe.wait_ge(rstt_saved, g)
                ins = pe.matmul(bank[NB][:, :], a_t[:, g % 2, t, :], xn[:, t, :], start=(t == 0), stop=(t == NT - 1))
                if t == NT - 1:
                    ins.then_inc(neigh_ps, 1)

            def turn_sums(g):
                pe.wait_ge(rst_ready, g + 1)
                for k in range(KD):
                    ins = pe.transpose(bank[NB][:, k * P:(k + 1) * P], rst[:, k * P:(k + 1) * P], ident[:, :])
                ins.then_inc(rstt_ps, 1)

            def graph(turn):
                if turn == FROM:
                    pe.wait_ge(edge_saved, 2)
                for what in pe_after[turn]:
                    {"pair": count_pair, "spare": count_spare, "sum": neighbours, "turn": turn_sums}[what[0]](*what[1:])

            for g, (which, p, b) in enumerate(projections):
                o, n = BLOCKS[b]
                c = (D if which == "k" else 0) + p * P
                if g >= 5:
                    pe.wait_ge(proj_saved, g - 4)
                for k in range(KD):
                    ins = pe.matmul(bank[g % 5][:, 0:n], w_qkv[:, k, c:c + P], xn_t[:, k, o:o + n],
                                    start=(k == 0), stop=(k == KD - 1))
                ins.then_inc(proj_ps, 1)
                lay_out_edges(g - PREP)
                graph(g)
            pe.wait_ge(proj_saved, NPROJ)
            for t in range(NT):
                if t >= 5:
                    pe.wait_ge(v_lo_ready, t - 4)
                for k in range(KD):
                    ins = pe.matmul(bank[(NPROJ + t) % 5][:, :], xn_t[:, k, t * P:(t + 1) * P], w_qkv[:, k, 2 * D:3 * D],
                                    start=(k == 0), stop=(k == KD - 1))
                ins.then_inc(proj_ps, 1)
                graph(NPROJ + t)
            pe.wait_ge(v_lo_ready, NT)

            def scores(s):
                h, b, t = steps[s]
                o, n = BLOCKS[b]
                kt = rows(t)
                if s >= NQB:
                    pe.wait_ge(p_lo_ready, s - NQB + 1)
                if s % SPH == 0:
                    pe.wait_ge(head_split, h + 1)
                    pe.wait_ge(head_ready[h], 48)
                for first, q in ((True, q_hi), (False, q_lo)):
                    ins = pe.matmul(bank[s % NQB][0:kt, 0:n], k_hl[h % 2][:, t * P:t * P + kt], q[h % 2][:, o:o + n],
                                    start=first, stop=not first)
                ins.then_inc(qk_ps, 1)

            scores(0)
            scores(1)
            for s, (h, b, t) in enumerate(steps):
                if s + 2 < NS:
                    scores(s + 2)
                n = BLOCKS[b][1]
                kt = rows(t)
                m = s // NT
                if t == 0 and m >= 2:
                    pe.wait_ge(av_saved, m - 1)
                pe.wait_ge(p_hi_ready, s + 1)
                pe.matmul(bank[AV + m % 2][:, 0:n], v_hl[0:kt, t, h, :, :], p_hi[0:kt, s % NPB, 0:n],
                          start=(t == 0), stop=False)
                pe.wait_ge(p_lo_ready, s + 1)
                pe.matmul(bank[AV + m % 2][:, 0:n], v_hl[0:kt, t, h, :, :], p_lo[0:kt, s % NPB, 0:n],
                          start=False, stop=(t == NT - 1)).then_inc(av_step, 1)
                graph(NPRE + s)

            pe.wait_ge(wo_in, 16)
            pe.wait_ge(rstt_saved, NT)
            for t in range(NT):
                r = rows(t)
                pe.wait_ge(av_saved, SPH * HEADS // NT - len(BLOCKS)
                           + sum(1 for o, n in BLOCKS if o < t * P + r))
                if t >= 8:
                    pe.wait_ge(out_added, t - 7)
                for p in range(PAIRS):
                    ins = pe.matmul(bank[(5 + t) % 8][0:r, :], q_t[:, p, t * P:t * P + r], w_o[:, p, :],
                                    start=(p == 0), stop=(p == PAIRS - 1))
                ins.then_inc(out_ps, 1)

            def mix(t, first, hidden):
                r = rows(t)
                c = (t - first) * P
                if t >= 2:
                    pe.wait_ge(x2_ready, t - 1)
                for m in range(KH):
                    if t == first:
                        pe.wait_ge(hid_lo, hidden + m + 1)
                    for i, (h, w) in enumerate(((h_hi, w2_hi(m)), (h_lo, w2_hi(m)), (h_hi, w2_lo[:, m, :]))):
                        ins = pe.matmul(bank[4 + t % 2][0:r, :], h[:, m, c:c + r], w,
                                        start=(m == 0 and i == 0), stop=(m == KH - 1 and i == 2))
                ins.then_inc(mix_ps, 1)

            def turn_x2n(t):
                pe.wait_ge(x2n_ready, t + 1)
                if t:
                    pe.wait_ge(x2nt_saved, t)
                for k in range(KD):
                    ins = pe.transpose(bank[6][:, k * P:(k + 1) * P], x2n[:, t, k * P:(k + 1) * P], ident[:, :])
                ins.then_inc(x2nt_ps, 1)

            def route(t):
                pe.wait_ge(x2nt_saved, t + 1)
                for k in range(KD):
                    ins = pe.matmul(bank[7][:, t * EXP:(t + 1) * EXP], x2n_t[:, t % 2, k, :], rw_sb[:, k, :],
                                    start=(k == 0), stop=(k == KD - 1))
                ins.then_inc(logit_ps, 1)

            pe.wait_ge(w1_in, 16)
            pe.wait_ge(rw_in, 16)
            g = 0
            for tiles in FC_TILES:
                o = tiles[0] * P
                n = min(N, tiles[-1] * P + P) - o
                for m in range(KH):
                    if g < 4:
                        pe.wait_ge(out_added, 4 + g)
                    else:
                        pe.wait_ge(hid_hi, g - 3)
                    for k in range(KD):
                        ins = pe.matmul(bank[g % 4][:, 0:n], w1[:, k, m * P:(m + 1) * P], rst_t[:, k, o:o + n],
                                        start=(k == 0), stop=(k == KD - 1))
                    ins.then_inc(hid_ps, 1)
                    g += 1
                    if o and m == 1:
                        turn_x2n(tiles[0] - 1)
                        route(tiles[0] - 2)
                    if o and m == 3:
                        route(tiles[0] - 1)
                pe.wait_ge(w2_lo_ready, KH)
                pe.wait_ge(out_added, NT)
                for t in tiles:
                    mix(t, tiles[0], g - KH)
                    if t - 1 in tiles:
                        turn_x2n(t - 1)
                    if t - 2 in tiles:
                        route(t - 2)
            turn_x2n(NT - 1)
            route(NT - 2)
            route(NT - 1)
            pe.wait_ge(mask_ready, 1)
            pe.matmul(bank[2][:, 0:NT * EXP], tri[:, :], mask16[:, :], start=True, stop=False, skip_group_check=True)
            for d in range(1, NT):
                pe.matmul(bank[2][:, d * EXP:NT * EXP], ones[:, :], mask16[:, 0:(NT - d) * EXP],
                          start=False, stop=(d == NT - 1), skip_group_check=True)
            for t in range(NT):
                ins = pe.matmul(bank[3][:, 0:EXP], ones[:, :], mask16[:, t * EXP:(t + 1) * EXP],
                                start=(t == 0), stop=(t == NT - 1))
            ins.then_inc(rank_ps, 1)
            pe.wait_ge(gates_ready, 1)
            for t in range(NT):
                if t >= 2:
                    pe.wait_ge(gt_saved, t - 1)
                pe.transpose(bank[t % 2][0:EXP, 0:P], gates[:, t, :], ident[:, :]).then_inc(gt_ps, 1)
            pe.wait_ge(route_ready, 1)
            pe.wait_ge(b2_in, 16)
            for t in range(NT):
                r = rows(t)
                pe.wait_ge(gt_saved, t + 1)
                if t >= 2:
                    pe.wait_ge(gb_added, t - 1)
                pe.matmul(bank[2 + t % 2][0:r, :], gates_t[:, t * P:t * P + r], b2_sb[:, :],
                          start=True, stop=True).then_inc(gb_ps, 1)
            pe.wait_ge(gb_added, NT)

            def turn_rows(a):
                for k in range(KD):
                    ins = pe.transpose(bank[4 + a][:, k * P:(k + 1) * P], xg[:, a, k * P:(k + 1) * P], ident[:, :])
                ins.then_inc(xgt_ps[a], 1)

            for a in range(2):
                pe.wait_ge(xg_in[a], 16)
                turn_rows(a)
            n = pe.value_load(npair[0:1, 0:1], min_val=1, max_val=(MAXT - 3) // 2)
            with pe.Fori(0, n) as j:
                e = [pe.value_load(te[0:1, bass.ds(2 * j + a, 1)], min_val=0, max_val=EXP - 1) for a in range(2)]
                for a in range(2):
                    pe.wait_ge(w_ready, e[a] + 1)
                    pe.wait_ge(xgt_saved[a], j + 1)
                    pe.wait_ge(hb_ready[a], j + 1)
                    for k in range(KD):
                        ins = pe.matmul(bank[a][:, 0:DFF], xg_t[:, a, k, :],
                                        arena[:, bass.ds(e[a] * EW + E_BASE + k * DFF, DFF)],
                                        start=(k == 0), stop=(k == KD - 1))
                    ins.then_inc(h_ps[a], 1)

                def turn_hidden(a):
                    pe.wait_ge(hg_ready[a], j + 1)
                    pe.wait_ge(hgt_saved[a], j + 1)
                    for k in range(KF):
                        ins = pe.transpose(bank[2 + a][:, k * P:(k + 1) * P], hg[:, a, k * P:(k + 1) * P], ident[:, :])
                    ins.then_inc(hgt_ps[a], 1)

                turn_hidden(0)
                for a in range(2):
                    pe.wait_ge(xg_in[a], 16 * (j + 2))
                    pe.wait_ge(xgt_saved[a], j + 1)
                    turn_rows(a)
                turn_hidden(1)
                for a in range(2):
                    pe.wait_ge(hgt_saved[a], j + 2)
                    pe.wait_ge(y_saved[a], j + 1)
                    for k in range(KF):
                        ins = pe.matmul(bank[6 + a][:, :], hg_t[:, a, k, :],
                                        arena[:, bass.ds(e[a] * EW + E_BASE + KD * DFF + k * D, D)],
                                        start=(k == 0), stop=(k == KF - 1))
                    ins.then_inc(y_ps[a], 1)


def kernel(x, src, dst, L0_gnn_W1, L0_gnn_b1, L0_gnn_W2, L0_gnn_b2, L0_gnn_eps, L0_mix_W_qkv, L0_mix_W_out,
           L0_mix_b_out, L0_ffn_router_w, L0_ffn_router_b, L0_ffn_w1, L0_ffn_b1, L0_ffn_w2, L0_ffn_b2):
    import numpy as np
    import concourse.bacc as bacc
    from concourse.bass_utils import run_bass_kernel_spmd

    def by_partition(w):
        w = np.asarray(w)
        return np.ascontiguousarray(w.reshape(-1, P, w.shape[1]).transpose(1, 0, 2))

    w1t = np.asarray(L0_ffn_w1).transpose(0, 2, 1).reshape(EXP, KD, P, DFF).transpose(0, 2, 1, 3).reshape(EXP, P, -1)
    w2t = np.asarray(L0_ffn_w2).transpose(0, 2, 1).reshape(EXP, KF, P, D).transpose(0, 2, 1, 3).reshape(EXP, P, -1)
    arrays = {
        "x": x, "src": src, "dst": dst,
        "wqkv": by_partition(np.asarray(L0_mix_W_qkv).T), "wo": by_partition(np.asarray(L0_mix_W_out).T),
        "bo": L0_mix_b_out, "gw1": by_partition(L0_gnn_W1), "gb1": np.asarray(L0_gnn_b1).reshape(KH, P).T,
        "gw2": by_partition(L0_gnn_W2), "gb2": L0_gnn_b2, "geps": L0_gnn_eps,
        "rw": by_partition(np.asarray(L0_ffn_router_w).T), "rb": L0_ffn_router_b,
        "ew": np.concatenate([w1t, w2t], axis=2), "eb1": np.asarray(L0_ffn_b1).reshape(-1), "eb2": L0_ffn_b2,
    }
    arrays = {f"in_{k}": np.ascontiguousarray(a) for k, a in arrays.items()}
    nc = bacc.Bacc("TRN2", target_bir_lowering=False, num_devices=1)
    args = [nc.dram_tensor(k, a.shape, mybir.dt.from_np(a.dtype), kind="ExternalInput").ap() for k, a in arrays.items()]
    out = nc.dram_tensor("out", (N, D), mybir.dt.float32, kind="ExternalOutput").ap()
    layer(nc, *args, out)
    r = run_bass_kernel_spmd(nc, [arrays], core_ids=[0])
    return r.results[0]["out"]
```
